# Optimizing a Trainium2 kernel written in Bass

```python
import numpy as np
import jax
import jax.numpy as jnp

def _softmax(x, axis=-1):
    return jax.nn.softmax(x, axis=axis)

def _gelu(x):
    return jax.nn.gelu(x, approximate=True)

def _silu(x):
    return jax.nn.silu(x)

def _sigmoid(x):
    return jax.nn.sigmoid(x)

def _layernorm(x, axis=-1, eps=1e-05):
    m = jnp.mean(x, axis=axis, keepdims=True)
    v = jnp.var(x, axis=axis, keepdims=True)
    return (x - m) / jnp.sqrt(v + eps)

def _scatter_add(tgt, idx, src, axis=0):
    return tgt.at[idx].add(src)

def _segment_sum(src, seg, n):
    return jax.ops.segment_sum(src, seg, n)
kernel_name = 'mk_hybrid_d1_jaxref_r8_621e21'

def setup_inputs(seed: int=0):
    np.random.seed(seed)
    _w = jnp.asarray

    def _L0_attn_a_setup():
        import math
        import jax, jax.numpy as jnp
        import numpy as np
        from jax.scipy.special import xlogy, gammaln

        def get_positional_embed(seq_len, feature_size):
            distances = jnp.arange(-seq_len + 1, seq_len, dtype=jnp.float32)
            n = feature_size // 6
            absd = jnp.abs(distances)[:, None]
            max_range = math.log(seq_len) / math.log(2.0)
            half_life = 2.0 ** jnp.linspace(3.0, max_range, n)
            feat_exp = jnp.exp(-math.log(2.0) / half_life[None, :] * absd)
            center_widths = 2.0 ** jnp.arange(1, n + 1, dtype=jnp.float32) - 1.0
            feat_cm = (center_widths[None, :] > absd).astype(jnp.float32)
            stddev = seq_len / (2.0 * n)
            start_mean = seq_len / n
            mean = jnp.linspace(start_mean, float(seq_len), n)[None, :]
            conc = (mean / stddev) ** 2
            rate = mean / stddev ** 2
            log_unnorm = xlogy(conc - 1.0, absd) - rate * absd
            log_norm = gammaln(conc) - conc * jnp.log(rate)
            probs = jnp.exp(log_unnorm - log_norm) + 1e-08
            feat_gamma = probs / jnp.max(probs, axis=-1, keepdims=True)
            emb = jnp.concatenate([feat_exp, feat_cm, feat_gamma], axis=-1)
            emb = jnp.concatenate([emb, jnp.sign(distances)[:, None] * emb], axis=-1)
            return emb

        def relative_shift(x):
            b, h, t1, t2m1 = x.shape
            x = jnp.pad(x, ((0, 0), (0, 0), (0, 0), (1, 0)))
            t2 = t2m1 + 1
            x = x.reshape(b, h, t2, t1)
            x = x[:, :, 1:, :]
            x = x.reshape(b, h, t1, t2 - 1)
            return x[..., :(t2 + 1) // 2]
        key = jax.random.key(seed)
        ks = jax.random.split(key, 9)
        B, L, D = (2, 128, 128)
        H, Dk, Dv = (8, 128, 128)
        R = 192
        sq = math.sqrt(2.0 / (D + Dk))
        sv = math.sqrt(2.0 / (D + Dv))
        return {'q': jax.random.normal(ks[0], (B, L, D), jnp.float32), 'w_qs': jax.random.normal(ks[1], (D, H * Dk), jnp.float32) * sq, 'w_ks': jax.random.normal(ks[2], (D, H * Dk), jnp.float32) * sq, 'w_vs': jax.random.normal(ks[3], (D, H * Dv), jnp.float32) * sv, 'w_rel_pos_k': jax.random.normal(ks[4], (R, H * Dk), jnp.float32) * 0.05, 'rel_embed_bias': jax.random.normal(ks[5], (1, H, 1, Dk), jnp.float32), 'rel_pos_bias': jax.random.normal(ks[6], (1, H, 1, Dk), jnp.float32), 'w_out': jax.random.normal(ks[7], (H * Dv, D), jnp.float32) * 0.02, 'b_out': jax.random.normal(ks[8], (D,), jnp.float32) * 0.02}
    _L0_attn_a_in = _L0_attn_a_setup()

    def _L0_attn_b_setup():
        import jax, jax.numpy as jnp
        import numpy as np
        D_MODEL = 128
        NUM_HEADS = 16
        HEAD_DIM = D_MODEL // NUM_HEADS
        B, T = (2, 256)
        key = jax.random.key(seed)
        ks = jax.random.split(key, 5)
        s_in = 1.0 / np.sqrt(D_MODEL)
        return {'x': jax.random.normal(ks[0], (B, T, D_MODEL), dtype=jnp.float32), 'Wq': jax.random.normal(ks[1], (D_MODEL, D_MODEL), dtype=jnp.float32) * s_in, 'bq': jnp.zeros((D_MODEL,), dtype=jnp.float32), 'Wk': jax.random.normal(ks[2], (D_MODEL, HEAD_DIM), dtype=jnp.float32) * s_in, 'bk': jnp.zeros((HEAD_DIM,), dtype=jnp.float32), 'Wv': jax.random.normal(ks[3], (D_MODEL, HEAD_DIM), dtype=jnp.float32) * s_in, 'bv': jnp.zeros((HEAD_DIM,), dtype=jnp.float32), 'Wo': jax.random.normal(ks[4], (D_MODEL, D_MODEL), dtype=jnp.float32) * s_in, 'bo': jnp.zeros((D_MODEL,), dtype=jnp.float32)}
    _L0_attn_b_in = _L0_attn_b_setup()

    def _L0_ffn_setup():
        import jax, jax.numpy as jnp
        import numpy as np
        TOP_K = 2
        EPS = 1e-09
        key = jax.random.key(seed)
        ks = jax.random.split(key, 6)
        B, T, D, H, E = (4, 256, 128, 256, 8)
        x = jax.random.normal(ks[0], (B, T, D), dtype=jnp.float32)
        Wg = jax.random.normal(ks[1], (E, D), dtype=jnp.float32) * 0.02
        W1 = jax.random.normal(ks[2], (E, 2 * H, D), dtype=jnp.float32) * 0.02
        b1 = jax.random.normal(ks[3], (E, 2 * H), dtype=jnp.float32) * 0.02
        Wo = jax.random.normal(ks[4], (D, H), dtype=jnp.float32) * 0.02
        bo = jax.random.normal(ks[5], (D,), dtype=jnp.float32) * 0.02
        return {'x': x, 'Wg': Wg, 'W1': W1, 'b1': b1, 'Wo': Wo, 'bo': bo}
    _L0_ffn_in = _L0_ffn_setup()
    _d = {'L0_attn_a_q': _L0_attn_a_in['q'], 'L0_attn_a_w_qs': _L0_attn_a_in['w_qs'], 'L0_attn_a_w_ks': _L0_attn_a_in['w_ks'], 'L0_attn_a_w_vs': _L0_attn_a_in['w_vs'], 'L0_attn_a_w_rel_pos_k': _L0_attn_a_in['w_rel_pos_k'], 'L0_attn_a_rel_embed_bias': _L0_attn_a_in['rel_embed_bias'], 'L0_attn_a_rel_pos_bias': _L0_attn_a_in['rel_pos_bias'], 'L0_attn_a_w_out': _L0_attn_a_in['w_out'], 'L0_attn_a_b_out': _L0_attn_a_in['b_out'], 'L0_attn_b_Wq': _L0_attn_b_in['Wq'], 'L0_attn_b_bq': _L0_attn_b_in['bq'], 'L0_attn_b_Wk': _L0_attn_b_in['Wk'], 'L0_attn_b_bk': _L0_attn_b_in['bk'], 'L0_attn_b_Wv': _L0_attn_b_in['Wv'], 'L0_attn_b_bv': _L0_attn_b_in['bv'], 'L0_attn_b_Wo': _L0_attn_b_in['Wo'], 'L0_attn_b_bo': _L0_attn_b_in['bo'], 'L0_ffn_Wg': _L0_ffn_in['Wg'], 'L0_ffn_W1': _L0_ffn_in['W1'], 'L0_ffn_b1': _L0_ffn_in['b1'], 'L0_ffn_Wo': _L0_ffn_in['Wo'], 'L0_ffn_bo': _L0_ffn_in['bo']}
    _x0 = _d['L0_attn_a_q']
    _d['L0_attn_a_q'] = jax.random.normal(jax.random.fold_in(jax.random.key(seed), 1), (4, 1024, 128), dtype=_x0.dtype)
    del _x0
    return _d

def reference(L0_attn_a_q, L0_attn_a_w_qs, L0_attn_a_w_ks, L0_attn_a_w_vs, L0_attn_a_w_rel_pos_k, L0_attn_a_rel_embed_bias, L0_attn_a_rel_pos_bias, L0_attn_a_w_out, L0_attn_a_b_out, L0_attn_b_Wq, L0_attn_b_bq, L0_attn_b_Wk, L0_attn_b_bk, L0_attn_b_Wv, L0_attn_b_bv, L0_attn_b_Wo, L0_attn_b_bo, L0_ffn_Wg, L0_ffn_W1, L0_ffn_b1, L0_ffn_Wo, L0_ffn_bo):

    def _L0_attn_a_ref(q, w_qs, w_ks, w_vs, w_rel_pos_k, rel_embed_bias, rel_pos_bias, w_out, b_out):
        import math
        import jax, jax.numpy as jnp
        import numpy as np
        from jax.scipy.special import xlogy, gammaln

        def get_positional_embed(seq_len, feature_size):
            distances = jnp.arange(-seq_len + 1, seq_len, dtype=jnp.float32)
            n = feature_size // 6
            absd = jnp.abs(distances)[:, None]
            max_range = math.log(seq_len) / math.log(2.0)
            half_life = 2.0 ** jnp.linspace(3.0, max_range, n)
            feat_exp = jnp.exp(-math.log(2.0) / half_life[None, :] * absd)
            center_widths = 2.0 ** jnp.arange(1, n + 1, dtype=jnp.float32) - 1.0
            feat_cm = (center_widths[None, :] > absd).astype(jnp.float32)
            stddev = seq_len / (2.0 * n)
            start_mean = seq_len / n
            mean = jnp.linspace(start_mean, float(seq_len), n)[None, :]
            conc = (mean / stddev) ** 2
            rate = mean / stddev ** 2
            log_unnorm = xlogy(conc - 1.0, absd) - rate * absd
            log_norm = gammaln(conc) - conc * jnp.log(rate)
            probs = jnp.exp(log_unnorm - log_norm) + 1e-08
            feat_gamma = probs / jnp.max(probs, axis=-1, keepdims=True)
            emb = jnp.concatenate([feat_exp, feat_cm, feat_gamma], axis=-1)
            emb = jnp.concatenate([emb, jnp.sign(distances)[:, None] * emb], axis=-1)
            return emb

        def relative_shift(x):
            b, h, t1, t2m1 = x.shape
            x = jnp.pad(x, ((0, 0), (0, 0), (0, 0), (1, 0)))
            t2 = t2m1 + 1
            x = x.reshape(b, h, t2, t1)
            x = x[:, :, 1:, :]
            x = x.reshape(b, h, t1, t2 - 1)
            return x[..., :(t2 + 1) // 2]
        B, L, _ = q.shape
        H, Dk = (rel_embed_bias.shape[1], rel_embed_bias.shape[3])
        Dv = w_vs.shape[1] // H
        scale = Dk ** (-0.5)
        Q = (q @ w_qs).reshape(B, L, H, Dk).transpose(0, 2, 1, 3) * scale
        K = (q @ w_ks).reshape(B, L, H, Dk).transpose(0, 2, 1, 3)
        V = (q @ w_vs).reshape(B, L, H, Dv).transpose(0, 2, 1, 3)
        attn = jnp.einsum('bnqd,bnkd->bnqk', Q + rel_embed_bias, K)
        positions = get_positional_embed(L, w_rel_pos_k.shape[0])
        rel_k = (positions @ w_rel_pos_k).reshape(-1, H, Dk).transpose(1, 0, 2)
        attn_pos = jnp.einsum('bnqd,nkd->bnqk', Q + rel_pos_bias, rel_k)
        attn_pos = relative_shift(attn_pos)
        a = jax.nn.softmax(attn + attn_pos, axis=-1)
        out = jnp.einsum('bnqk,bnkd->bnqd', a, V)
        out = out.transpose(0, 2, 1, 3).reshape(B, L, H * Dv)
        return out @ w_out + b_out

    def _L0_attn_b_ref(x, Wq, bq, Wk, bk, Wv, bv, Wo, bo):
        import jax, jax.numpy as jnp
        import numpy as np
        D_MODEL = 128
        NUM_HEADS = 16
        HEAD_DIM = D_MODEL // NUM_HEADS
        B, T = (2, 256)
        b, t, _ = x.shape
        q = x @ Wq + bq
        k = x @ Wk + bk
        v = x @ Wv + bv
        q = q.reshape(b, t, NUM_HEADS, HEAD_DIM)
        scores = jnp.einsum('bthd,bsd->bhts', q, k) / jnp.sqrt(jnp.float32(HEAD_DIM))
        mask = jnp.tril(jnp.ones((t, t), dtype=scores.dtype))
        scores = scores * mask - 10000000000.0 * (1.0 - mask)
        probs = jax.nn.softmax(scores, axis=-1)
        out = jnp.einsum('bhts,bsd->bthd', probs, v)
        out = out.reshape(b, t, NUM_HEADS * HEAD_DIM)
        return out @ Wo + bo

    def _L0_ffn_ref(x, Wg, W1, b1, Wo, bo):
        import jax, jax.numpy as jnp
        import numpy as np
        TOP_K = 2
        EPS = 1e-09
        E = Wg.shape[0]
        gate_logits = jnp.einsum('btd,ed->bte', x, Wg)
        gate_scores = jax.nn.softmax(gate_logits, axis=-1)
        topk_val, topk_idx = jax.lax.top_k(gate_scores, TOP_K)
        topk_val = topk_val / (topk_val.sum(axis=-1, keepdims=True) + EPS)
        comb = (jax.nn.one_hot(topk_idx, E, dtype=x.dtype) * topk_val[..., None]).sum(axis=-2)
        out = jnp.zeros_like(x)
        for e in range(E):
            h = jnp.einsum('btd,hd->bth', x, W1[e]) + b1[e]
            a, b = jnp.split(h, 2, axis=-1)
            g = a * jax.nn.sigmoid(b)
            eo = jnp.einsum('bth,dh->btd', g, Wo) + bo
            out = out + eo * comb[..., e:e + 1]
        return out
    x = L0_attn_a_q
    x = x + _L0_attn_a_ref(_layernorm(x, axis=-1), L0_attn_a_w_qs, L0_attn_a_w_ks, L0_attn_a_w_vs, L0_attn_a_w_rel_pos_k, L0_attn_a_rel_embed_bias, L0_attn_a_rel_pos_bias, L0_attn_a_w_out, L0_attn_a_b_out)
    x = x + _L0_ffn_ref(_layernorm(x, axis=-1), L0_ffn_Wg, L0_ffn_W1, L0_ffn_b1, L0_ffn_Wo, L0_ffn_bo)
    x = x + _L0_attn_b_ref(_layernorm(x, axis=-1), L0_attn_b_Wq, L0_attn_b_bq, L0_attn_b_Wk, L0_attn_b_bk, L0_attn_b_Wv, L0_attn_b_bv, L0_attn_b_Wo, L0_attn_b_bo)
    x = x + _L0_ffn_ref(_layernorm(x, axis=-1), L0_ffn_Wg, L0_ffn_W1, L0_ffn_b1, L0_ffn_Wo, L0_ffn_bo)
    return x

_drawn_inputs = setup_inputs


def setup_inputs(seed=0):
    import zlib

    import numpy as np

    out = dict(_drawn_inputs(seed))
    spreads = {'L0_attn_b_bq': (0.0, 0.8),
     'L0_attn_b_bk': (0.0, 0.8),
     'L0_attn_b_bv': (0.0, 0.1),
     'L0_attn_b_bo': (0.0, 0.1)}
    factors = {'L0_attn_a_b_out': 2.892, 'L0_ffn_b1': 8.0}
    for name, (base, spread) in spreads.items():
        noise = np.random.default_rng([zlib.crc32(name.encode()), seed]).standard_normal(out[name].shape)
        drawn = base * np.exp(spread * noise) if base else spread * noise
        out[name] = jnp.asarray(drawn.astype(out[name].dtype))
    for name, factor in factors.items():
        out[name] = (out[name] * factor).astype(out[name].dtype)
    return out
```

```python
import math
from contextlib import ExitStack

import numpy as np
import concourse.bass as bass
from concourse import mybir
from concourse.alu_op_type import AluOpType as ALU

F32 = mybir.dt.float32
F32R = mybir.dt.float32r
BF16 = mybir.dt.bfloat16
U32 = mybir.dt.uint32
ACT = mybir.ActivationFunctionType
AX = mybir.AxisListType.X

B, L, D = 4, 1024, 128
NT = B * L // 128
H, DK = 8, 128
NF = 96
E, FH = 8, 256
HB, DB = 16, 8
EPS_LN = 1e-5
EPS_TOPK = 1e-9
RW = 1152
NEG = -1e30


class Token:

    def __init__(self, sem=None, value=None):
        self.sem, self.value, self.used = sem, value, sem is not None


class Queue:

    def __init__(self, sem):
        self.sem, self.items = sem, []

    def op(self, emit, *waits):
        flat = []
        for w in waits:
            flat += w if isinstance(w, (list, tuple)) else [w]
        flat = [w for w in flat if w is not None]
        for w in flat:
            w.used = True
        t = Token()
        self.items.append((flat, emit, t))
        return t

    def last(self):
        return [i[2] for i in self.items[-1:]]

    def number(self):
        n = 0
        for _, _, t in self.items:
            if t.sem is None and t.used:
                n += 1
                t.sem, t.value = self.sem, n

    def play(self, eng):
        seen = {}
        for waits, emit, t in self.items:
            need = {}
            for w in waits:
                if w.value > seen.get(w.sem.name, (None, 0))[1]:
                    if w.value > need.get(w.sem.name, (None, 0))[1]:
                        need[w.sem.name] = (w.sem, w.value)
            for name, (s, v) in need.items():
                eng.wait_ge(s, v)
                seen[name] = (s, v)
            ins = emit(eng)
            if t.sem is self.sem and t.used:
                ins.then_inc(self.sem, 1)


class DmaSem:

    def __init__(self, sem):
        self.sem, self.value = sem, 0

    def start(self, queue, out, in_, *waits):
        self.value += 16
        t = Token(self.sem, self.value)
        queue.op(lambda e: e.dma_start(out, in_).then_inc(self.sem, 16), *waits)
        return t


class Program:
    def __init__(self, nc, dram):
        self.nc, self.dr = nc, dram
        self.ctx = ExitStack()

    def sem(self, name):
        return self.ctx.enter_context(self.nc.semaphore(name))

    def fence(self):
        t = []
        for q in (self.pe, self.act, self.dve, self.pool):
            t += q.last()
        return t + self.dma_tokens

    def dma(self, out, in_, *waits, sem=None):
        if sem is None:
            sem = DmaSem(self.sem(f"dma{self.ndma}"))
            self.ndma += 1
        t = sem.start(self.sp, out, in_, *waits)
        return t

    def build(self):
        nc = self.nc
        with self.ctx:
            self.pe, self.act, self.dve, self.pool, self.sp = (
                Queue(self.sem("s_" + n)) for n in ("pe", "act", "dve", "pool", "sp"))
            self.ndma, self.dma_tokens = 0, []
            keep = self.ctx
            self.ps = keep.enter_context(nc.psum_tensor("ps", [128, 8, 512], F32))
            self.x = keep.enter_context(nc.sbuf_tensor("x", [128, NT, 128], F32))
            self.ident = keep.enter_context(nc.sbuf_tensor("ident", [128, 128], F32))
            self.identb = keep.enter_context(nc.sbuf_tensor("identb", [128, 128], BF16))
            self.maskq = keep.enter_context(nc.sbuf_tensor("maskq", [128, 128], BF16))
            self.maskk = keep.enter_context(nc.sbuf_tensor("maskk", [128, 128], BF16))
            self.ones = keep.enter_context(nc.sbuf_tensor("ones", [128, 128], F32R))
            self.iota = keep.enter_context(nc.sbuf_tensor("iota", [128, E], F32))
            self.negrow = keep.enter_context(nc.sbuf_tensor("negrow", [128, 1], F32))
            self.lowmask = keep.enter_context(nc.sbuf_tensor("lowmask", [128, 2], F32))
            self.constants()
            xin = self.dr["q"].rearrange("(n p) d -> p n d", p=128)
            self.t_x = [self.dma(self.x[:, 8 * b:8 * b + 8, :], xin[:, 8 * b:8 * b + 8, :]) for b in range(B)]
            xo = self.dr["out"].rearrange("(n p) d -> p n d", p=128)

            self.attention_a()
            self.ffn()
            self.attention_b()
            self.ffn()
            s_out = DmaSem(self.sem("s_out"))
            f = self.fence()
            t = s_out.start(self.sp, xo, self.x[:, :, :], f)
            self.sp.op(lambda e: e.wait_ge(t.sem, t.value))

            for q in (self.pe, self.act, self.dve, self.pool, self.sp):
                q.number()
            block = self.ctx.enter_context(nc.Block())
            block.sync(lambda e: self.sp.play(e))
            block.tensor(lambda e: self.pe.play(e))
            block.scalar(lambda e: self.act.play(e))
            block.vector(lambda e: self.dve.play(e))
            block.gpsimd(lambda e: self.pool.play(e))

    def constants(self):
        p = self.pool
        cond = dict(pattern=[[-1, 128]], channel_multiplier=1, base=0)
        a = p.op(lambda e: e.memset(self.ident[:, :], 0.0))
        b = p.op(lambda e: e.memset(self.identb[:, :], 0.0))
        c = p.op(lambda e: e.memset(self.maskq[:, :], 0.0))
        d = p.op(lambda e: e.memset(self.maskk[:, :], 0.0))
        self.t_ident = p.op(lambda e: e.affine_select(out=self.ident[:, :], in_=self.ident[:, :],
                            compare_op=ALU.not_equal, fill=1.0, **cond), a)
        p.op(lambda e: e.affine_select(out=self.identb[:, :], in_=self.identb[:, :],
             compare_op=ALU.not_equal, fill=1.0, **cond), b)
        p.op(lambda e: e.affine_select(out=self.maskq[:, :], in_=self.maskq[:, :],
             compare_op=ALU.is_ge, fill=NEG, **cond), c)
        p.op(lambda e: e.affine_select(out=self.maskk[:, :], in_=self.maskk[:, :], compare_op=ALU.is_ge,
             fill=NEG, pattern=[[1, 128]], channel_multiplier=-1, base=0), d)
        a = p.op(lambda e: e.memset(self.negrow[:, :], 0.0))
        self.t_neg = p.op(lambda e: e.affine_select(out=self.negrow[:, :], in_=self.negrow[:, :],
                          compare_op=ALU.not_equal, fill=-1.0, base=-1, pattern=[[0, 1]], channel_multiplier=1), a)
        a = self.dve.op(lambda e: e.memset(self.ones[:, :].bitcast(F32), 0.0))
        self.t_ones = self.dve.op(lambda e: e.memset(self.ones[0:2, :].bitcast(F32), 1.0), a)
        self.t_low = self.dma(self.lowmask[:, :], self.dr["low"])
        self.t_const = p.op(lambda e: e.iota(self.iota[:, :], pattern=[[1, E]], base=0, channel_multiplier=0,
                                             allow_small_or_imprecise_dtypes=True))

    def split(self, hi, lo, src, *waits, eng=None):
        a = self.act.op(lambda e: e.activation(hi, src, ACT.Copy), *waits)
        b = self.dve.op(lambda e: e.tensor_tensor(lo, src, hi.bitcast(F32), ALU.subtract), a)
        return [a, b]

    def mm3(self, e, out, lh, ll, rh, rl):
        e.matmul(out, lh, rh, start=True, stop=False)
        e.matmul(out, lh, rl, start=False, stop=False)
        return e.matmul(out, ll, rh, start=False, stop=True)

    def layernorm(self, ctx, xh, xl, start):
        nc, x = self.nc, self.x
        with ExitStack() as c:
            sb = lambda n, s, d: c.enter_context(nc.sbuf_tensor(f"ln{self.ndma}{n}", s, d))
            st = sb("st", [128, NT, 6], F32)
            mv = sb("mv", [128, NT, 2], F32)
            ve = sb("ve", [128, NT], F32)
            sd = sb("sd", [128, NT], F32)
            rs = sb("rs", [128, NT], F32)
            xn = sb("xn", [128, 4, 128], F32)
            self.ndma += 1
            for n in range(NT):
                t = self.dve.op(lambda e, n=n: e.bn_stats(st[:, n, :], x[:, n, :]), start(n))
            for n in range(NT):
                t2 = self.dve.op(lambda e, n=n: e.bn_aggr(mv[:, n, :], st[:, n, :]), t)
            t = self.dve.op(lambda e: e.tensor_scalar(ve[:, :], mv[:, :, 1], EPS_LN, None, ALU.add), t2)
            t = self.act.op(lambda e: e.activation(sd[:, :], ve[:, :], ACT.Sqrt), t)
            tr = self.dve.op(lambda e: e.reciprocal(rs[:, :], sd[:, :]), t)
            done, tp, lo = [], [None] * NT, [None, None]
            for n in range(NT):
                w = [tr] + ([tp[n - 4]] if n >= 4 else [])
                t = self.dve.op(lambda e, n=n: e.tensor_scalar(xn[:, n % 4, :], x[:, n, :], mv[:, n, 0:1],
                                rs[:, n:n + 1], ALU.subtract, ALU.mult), w)
                bank = (n // 4) % 2
                tp[n] = self.pe.op(lambda e, n=n, bank=bank: e.transpose(
                    self.ps[:, bank, 128 * (n % 4):128 * (n % 4) + 128], xn[:, n % 4, :], self.ident[:, :]),
                    t, lo[bank], self.t_ident, start(0))
                if n % 4 == 3:
                    cs = slice(128 * (n - 3), 128 * (n + 1))
                    hl = self.split(xh[:, cs], xl[:, cs], self.ps[:, bank, :], tp[n], start(0))
                    lo[bank] = hl[1]
                    done.append(hl)
            self.ln_end = self.dve.last() + self.act.last() + self.pe.last()
        return done

    def attention_a(self):
        nc, ps, x, dr = self.nc, self.ps, self.x, self.dr
        PE, AC, DV = self.pe, self.act, self.dve
        c = ExitStack()
        with c:
            sb = lambda n, s, d: c.enter_context(nc.sbuf_tensor("a_" + n, s, d))
            xh, xl = sb("xh", [128, B * L], F32R), sb("xl", [128, B * L], F32R)
            t_xn = self.layernorm(c, xh, xl, lambda n: self.t_x[n // 8])
            fh, fl = sb("fh", [NF, 2048], F32R), sb("fl", [NF, 2048], F32R)
            zh, zl = sb("zh", [NF, 2], F32R), sb("zl", [NF, 2], F32R)
            rh, rl = sb("rh", [128, 2048], F32R), sb("rl", [128, 2048], F32R)
            Kh, Kl = sb("Kh", [128, 2, L], F32R), sb("Kl", [128, 2, L], F32R)
            Vh, Vl = sb("Vh", [128, 2, L], F32R), sb("Vl", [128, 2, L], F32R)
            Qh, Ql = sb("Qh", [128, 2, 2, 512], F32R), sb("Ql", [128, 2, 2, 512], F32R)
            Ph, Pl = sb("Ph", [128, 8, 512], F32R), sb("Pl", [128, 8, 512], F32R)
            oh, ol = sb("oh", [128, 512], F32R), sb("ol", [128, 512], F32R)
            rt = sb("rt", [128, 2, RW], F32)
            sp = sb("sp", [128, 4, L], F32)
            wst = sb("wst", [128, 4, 128], F32)
            wh, wl = sb("wh", [128, 2, 4, 128], F32R), sb("wl", [128, 2, 4, 128], F32R)
            gst = sb("gst", [NF, 2, 128], F32)
            gsm = sb("gsm", [NF, 3, 128], F32)
            gh, gl = sb("gh", [NF, 2, 3, 128], F32R), sb("gl", [NF, 2, 3, 128], F32R)
            bias = sb("bias", [128, 2, H], F32)
            nm = sb("nm", [128, 8], F32)
            ls = sb("ls", [128, 16], F32)
            rv = sb("rv", [128, 8], F32)
            bo = rt[:, 0, 0:128]
            scr = nc.dram_tensor("scr", (4, 128, RW), F32, kind="Internal").ap()

            lnw = self.ln_end
            t_bo = self.dma(bo, bass.AP(dr["bo_a"].tensor, 0, [[0, 128], [1, 128]]), lnw)
            t_bias = self.dma(bias[:, :, :], dr["bias_a"].rearrange("d (a h) -> d a h", a=2), lnw)
            t_xb = DV.op(lambda e: e.tensor_tensor(x[:, :, :], x[:, :, :], bass.AP(
                bo.tensor, bo.offset, [bo.ap[0], [0, NT], [1, 128]]), ALU.add), t_bo, lnw)
            fst = sp[0:NF, 0:2, :].rearrange("p a n -> p (a n)")
            t_f = self.dma(fst, dr["feat"], lnw)
            zst = sp[0:NF, 2, 0:2]
            t_z = self.dma(zst, dr["feat0"], lnw)
            t_fs = self.split(fh[:, :], fl[:, :], fst, t_f) + self.split(zh[:, :], zl[:, :], zst, t_z)

            s_w, s_g = DmaSem(self.sem("s_w")), DmaSem(self.sem("s_g"))
            s_wr = [DmaSem(self.sem(f"s_wr{i}")) for i in range(4)]
            s_rd = [DmaSem(self.sem(f"s_rd{i}")) for i in range(4)]

            SC = float(DK) ** -0.5
            NTI = H * NT
            t_wt, t_out = {}, {}
            st_free = [None]

            def weights(h):
                s = h % 2
                free = [st_free[0], t_out.get(4 * 2 * h - 9)]
                hs = slice(128 * h, 128 * h + 128)
                for k, nme in enumerate(("w_qs", "w_ks", "w_vs")):
                    tw = s_w.start(self.sp, wst[:, k, :], dr[nme][:, hs], *free, lnw)
                tw = s_w.start(self.sp, wst[:, 3, :], dr["w_out"][hs, :])
                tg = s_g.start(self.sp, gst[:, :, :], dr["w_rel"][:, hs].rearrange("(a p) n -> p a n", p=NF), *free, lnw)
                a = DV.op(lambda e: e.tensor_scalar(wst[:, 0, :], wst[:, 0, :], SC, None, ALU.mult), tw)
                b = [DV.op(lambda e: e.tensor_tensor(gsm[:, 0, :], gst[:, 0, :], gst[:, 1, :], ALU.subtract), tg, free),
                     DV.op(lambda e: e.tensor_tensor(gsm[:, 1, :], gst[:, 0, :], gst[:, 1, :], ALU.add)),
                     DV.op(lambda e: e.tensor_copy(gsm[:, 2, :], gst[:, 1, :]))]
                r = self.split(wh[:, s, :, :], wl[:, s, :, :], wst[:, :, :], a, free)
                r += self.split(gh[:, s, :, :], gl[:, s, :, :], gsm[:, :, :], b, free)
                st_free[0] = r[-1]
                t_wt[h] = r

            XB = ps[:, 7, :]
            OB = ps[:, 6, :]
            xfree = [None]
            rbank_free, tb_free, s_free, o_free = [None, None], [None, None], [None], [None]
            t_rel, t_q, t_k, t_v = [None] * 8, {}, {}, {}
            pe_R, pe_S, pe_T, pe_PV, pe_OUT = {}, {}, {}, {}, {}
            t_rd, t_wd, t_add, t_exp, t_PT, t_lo = {}, {}, {}, {}, {}, {}
            rev = {}

            def relunit(h, u):
                s, cs = h % 2, slice(256 * u, 256 * u + 256)
                g = 0 if u < 4 else 1
                out = ps[:, 7, 0:256]

                def emit(e):
                    i = self.mm3(e, out, gh[:, s, g, :], gl[:, s, g, :], fh[:, cs], fl[:, cs])
                    if u == 3:
                        i = self.mm3(e, ps[:, 7, 256:258], gh[:, s, 2, :], gl[:, s, 2, :], zh[:, :], zl[:, :])
                    return i
                p = PE.op(emit, xfree[0], t_wt[h], t_fs)
                last = pe_R.get(max(pe_R)) if pe_R else None
                if u == 3:
                    fix = DV.op(lambda e: e.tensor_copy(rv[:, 6:7], ps[:, 7, 257:258]), p)
                    p = DV.op(lambda e: e.tensor_tensor(ps[:, 7, 255:256], ps[:, 7, 255:256], rv[:, 6:7], ALU.add), fix)
                t_rel[u] = self.split(rh[:, cs], rl[:, cs], out, p, last)
                xfree[0] = t_rel[u][1]

            def qunit(qd):
                h, s = qd // 8, qd % 2
                cols = slice(512 * (qd % 8), 512 * (qd % 8) + 512)
                p = PE.op(lambda e: self.mm3(e, XB, wh[:, h % 2, 0, :], wl[:, h % 2, 0, :], xh[:, cols], xl[:, cols]),
                          xfree[0], t_wt[h], t_xn[qd % 8])
                war = [pe_S.get(4 * qd - 5), pe_R.get(4 * qd - 5)]
                a = [AC.op(lambda e, k=k: e.activation(Qh[:, s, k, :], XB, ACT.Identity, bias=bias[:, k, h:h + 1]),
                           p, war, t_bias) for k in range(2)]
                d = [DV.op(lambda e, k=k: e.scalar_tensor_tensor(Ql[:, s, k, :], XB, bias[:, k, h:h + 1],
                           Qh[:, s, k, :].bitcast(F32), ALU.add, ALU.subtract), a) for k in range(2)]
                t_q[qd] = a + d
                xfree[0] = d[1]

            def kunit(bh, half):
                h, b, s = bh // B, bh % B, bh % 2
                cols = slice(L * b + 512 * half, L * b + 512 * half + 512)
                p = PE.op(lambda e: self.mm3(e, XB, wh[:, h % 2, 1, :], wl[:, h % 2, 1, :], xh[:, cols], xl[:, cols]),
                          xfree[0], t_wt[h], t_xn[2 * b + half])
                o = slice(512 * half, 512 * half + 512)
                r = self.split(Kh[:, s, o], Kl[:, s, o], XB, p, pe_S.get(8 * (bh - 1) - 1))
                t_k.setdefault(bh, []).extend(r)
                xfree[0] = r[1]

            def vunit(bh, half):
                h, b, s = bh // B, bh % B, bh % 2

                def emit(e):
                    for j in range(4):
                        cs = slice(L * b + 512 * half + 128 * j, L * b + 512 * half + 128 * j + 128)
                        i = self.mm3(e, ps[:, 7, 128 * j:128 * j + 128], xh[:, cs], xl[:, cs],
                                     wh[:, h % 2, 2, :], wl[:, h % 2, 2, :])
                    return i
                p = PE.op(emit, xfree[0], t_wt[h], t_xn[2 * b + half])
                o = slice(512 * half, 512 * half + 512)
                r = self.split(Vh[:, s, o], Vl[:, s, o], XB, p, pe_PV.get(2 * (bh - 1) - 1))
                t_v.setdefault(bh, []).extend(r)
                xfree[0] = r[1]

            def rtile(t):
                I, qd, s = t % 8, t // 4, (t // 4) % 2
                c0 = 896 - 128 * I
                qs = slice(128 * (t % 4), 128 * (t % 4) + 128)
                ev = []
                for k in range(3):
                    rb = (3 * t + k) % 2
                    cs = slice(c0 + 384 * k, c0 + 384 * k + 384)
                    units = [t_rel[u] for u in range(cs.start // 256, (cs.stop - 1) // 256 + 1)]
                    waits = [rbank_free[rb], t_q[qd]]
                    for u in units:
                        waits += u
                    p = PE.op(lambda e, rb=rb, cs=cs: self.mm3(e, ps[:, rb, 0:384], Qh[:, s, 1, qs], Ql[:, s, 1, qs],
                              rh[:, cs], rl[:, cs]), *waits)
                    dst = rt[:, t % 2, 384 * k:384 * k + 384]
                    src = ps[:, rb, 0:384]
                    war = [t_wd.get(t - 2), t_xb]
                    ev.append((p, dst, src, war, rb))
                    rev[t] = ev
                    if k < 2:
                        revac(t, k)
                pe_R[t] = p

            def revac(t, k):
                p, dst, src, war, rb = rev[t][k]
                if k == 1:
                    a = DV.op(lambda e: e.tensor_copy(dst, src), p, war)
                else:
                    a = AC.op(lambda e: e.activation(dst, src, ACT.Copy), p, war)
                rbank_free[rb] = a
                rev[t][k] = a

            def rwrite(t):
                t_wd[t] = s_wr[t % 4].start(self.sp, scr[t % 4, :, :], rt[:, t % 2, :], rev[t], t_rd.get(t - 4))

            def rread(t):
                src = bass.AP(scr.tensor, (t % 4) * 128 * RW + 127, [[RW - 1, 128], [1, L]])
                t_rd[t] = s_rd[t % 4].start(self.sp, sp[:, t % 4, :], src, t_wd[t], pe_T.get(t - 4), t_fs)

            def stile(t):
                bh, qd = t // 8, t // 4
                s, q2 = bh % 2, qd % 2
                qs = slice(128 * (t % 4), 128 * (t % 4) + 128)

                def emit(e):
                    for k in range(2):
                        cs = slice(512 * k, 512 * k + 512)
                        i = self.mm3(e, ps[:, 2 + k, :], Qh[:, q2, 0, qs], Ql[:, q2, 0, qs], Kh[:, s, cs], Kl[:, s, cs])
                    return i
                pe_S[t] = PE.op(emit, s_free[0], t_q[qd], t_k[bh])
                w = sp[:, t % 4, :]
                t_add[t] = DV.op(lambda e: e.tensor_tensor_reduce(
                    out=w, in0=ps[:, 2:4, :].rearrange("p a n -> p (a n)"), in1=w, scale=-1.0, scalar=3e38,
                    op0=ALU.add, op1=ALU.min, accum_out=nm[:, t % 8:t % 8 + 1]), pe_S[t], t_rd[t], t_exp.get(t - 8))
                s_free[0] = t_add[t]

            def softmax(t):
                w = sp[:, t % 4, :]
                t_exp[t] = AC.op(lambda e: e.activation(w, w, ACT.Exp, bias=nm[:, t % 8:t % 8 + 1], scale=-1.0,
                                 accum_out=ls[:, t % 16:t % 16 + 1]), t_add[t], t_out.get(t // 4 - 4))

            def ttile(t):
                w = sp[:, t % 4, :]
                r = []
                for k in range(2):
                    bank = 4 + k

                    def emit(e, k=k, bank=bank):
                        for j in range(4):
                            i = e.transpose(ps[:, bank, 128 * j:128 * j + 128],
                                            w[:, 512 * k + 128 * j:512 * k + 128 * j + 128], self.ident[:, :])
                        return i
                    p = PE.op(emit, t_exp[t], tb_free[k])
                    o = slice(128 * (t % 4), 128 * (t % 4) + 128)
                    src = ps[:, bank, :].rearrange("p (j n) -> p j n", j=4)
                    a, d = self.split(Ph[:, 4 * k:4 * k + 4, o], Pl[:, 4 * k:4 * k + 4, o], src, p, pe_PV.get(t // 4 - 1))
                    tb_free[k] = d
                    r += [a, d]
                pe_T[t] = p
                t_PT[t] = r

            def pv(qd):
                bh = qd // 2
                s = bh % 2

                def emit(e):
                    for j in range(8):
                        cs = slice(128 * j, 128 * j + 128)
                        e.matmul(OB, Vh[:, s, cs], Ph[:, j, :], start=j == 0, stop=False)
                        e.matmul(OB, Vh[:, s, cs], Pl[:, j, :], start=False, stop=False)
                        i = e.matmul(OB, Vl[:, s, cs], Ph[:, j, :], start=False, stop=j == 7)
                    return i
                pe_PV[qd] = PE.op(emit, *[t_PT[t] for t in range(4 * qd, 4 * qd + 4)], t_v[bh], o_free[0])
                r = self.split(oh[:, :], ol[:, :], OB, pe_PV[qd], pe_OUT.get(qd - 1))
                o_free[0] = r[1]
                t_lo[qd] = r

            def outproj(qd):
                h = qd // 8

                def emit(e):
                    for k in range(4):
                        cs = slice(128 * k, 128 * k + 128)
                        i = self.mm3(e, ps[:, 7, cs], oh[:, cs], ol[:, cs], wh[:, h % 2, 3, :], wl[:, h % 2, 3, :])
                    return i
                pe_OUT[qd] = PE.op(emit, t_lo[qd], xfree[0], t_wt[h])
                c4 = (4 * qd) % 16
                r = DV.op(lambda e: e.reciprocal(rv[:, 0:4], ls[:, c4:c4 + 4]), t_exp[4 * qd + 3], t_out.get(qd - 1))
                for k in range(4):
                    n = 4 * (qd % 8) + k
                    t = DV.op(lambda e, k=k, n=n: e.scalar_tensor_tensor(
                        x[:, n, :], ps[:, 7, 128 * k:128 * k + 128], rv[:, k:k + 1], x[:, n, :], ALU.mult, ALU.add),
                        r, pe_OUT[qd], t_xb)
                t_out[qd] = t
                xfree[0] = t

            weights(0)
            for u in (7, 6, 5, 4, 3, 2, 1, 0):
                relunit(0, u)
            qunit(0)
            for half in range(2):
                kunit(0, half)
                vunit(0, half)
            for t in range(3):
                rtile(t)
                revac(t, 2)
                rwrite(t)
                if t:
                    rread(t - 1)
            REL = {-1: (7,), 1: (6,), 3: (5,), 4: (4, 3), 6: (2,), 8: (1,), 10: (0,)}
            rel_at = {}
            for h in range(1, H):
                for ds, us in REL.items():
                    rel_at.setdefault(8 * (4 * h - 1) + ds, []).extend((h, u) for u in us)
            for s in range(NTI + 6):
                kq, qd, bh = s % 4, s // 4, s // 8
                live = s < NTI
                if live and s % 32 == 8 and s // 32 + 1 < H:
                    weights(s // 32 + 1)
                if live:
                    stile(s)
                if kq == 0 and qd + 1 < NTI // 4:
                    qunit(qd + 1)
                if s + 3 < NTI:
                    rtile(s + 3)
                if live:
                    softmax(s)
                if s + 3 < NTI:
                    revac(s + 3, 2)
                    rwrite(s + 3)
                if s + 2 < NTI:
                    rread(s + 2)
                if 0 < s <= NTI:
                    ttile(s - 1)
                if kq == 0 and 0 < qd <= NTI // 4:
                    pv(qd - 1)
                if kq == 1 and 0 < qd <= NTI // 4:
                    outproj(qd - 1)
                if live and kq == 1 and bh + 1 < NTI // 8:
                    kunit(bh + 1, qd % 2)
                if live and kq == 2 and bh + 1 < NTI // 8:
                    vunit(bh + 1, qd % 2)
                for h, u in rel_at.get(s, ()):
                    relunit(h, u)
            self.dma_tokens = list(t_wd.values())[-4:] + list(t_rd.values())[-4:]

    def ffn(self):
        nc, ps, x, dr = self.nc, self.ps, self.x, self.dr
        PE, AC, DV = self.pe, self.act, self.dve
        f0 = self.fence()
        tag = f"f{self.ndma}_"
        c = ExitStack()
        with c:
            sb = lambda n, s, d: c.enter_context(nc.sbuf_tensor(tag + n, s, d))
            xh, xl = sb("xh", [128, B * L], F32R), sb("xl", [128, B * L], F32R)
            Wh, Wl = sb("Wh", [128, E, 512], F32R), sb("Wl", [128, E, 512], F32R)
            bs = sb("bs", [128, E, 512], F32R)
            wst = sb("wst", [128, E, 512], F32)
            gst = sb("gst", [128, E], F32)
            gh, gl = sb("gh", [128, E], F32R), sb("gl", [128, E], F32R)
            ost = sb("ost", [128, 2, 128], F32)
            oh, ol = sb("oh", [128, 2, 128], F32R), sb("ol", [128, 2, 128], F32R)
            bo = sb("bo", [128, 128], F32)
            lg = sb("lg", [128, NT, E], F32)
            ex = sb("ex", [128, NT, E], F32)
            v8 = sb("v8", [128, NT, 8], F32)
            i8 = sb("i8", [128, NT, 8], U32)
            if8 = sb("if8", [128, NT, 2], F32)
            sm = sb("sm", [128, NT], F32)
            pv = sb("pv", [128, NT, 2], F32)
            den = sb("den", [128, NT], F32)
            oht = sb("oht", [128, NT, E], F32)
            comb = sb("comb", [128, NT, E], F32)
            csum = sb("csum", [128, NT], F32)
            sig = sb("sig", [128, 4, FH], F32)
            gt = sb("gt", [128, 2, FH], F32)
            acc = sb("acc", [128, 2, FH], F32)
            th, tl = sb("th", [128, 2, FH], F32R), sb("tl", [128, 2, FH], F32R)

            tw = self.dma(wst[:, :, :], dr["w1t"].rearrange("d (e h) -> d e h", e=E), f0)
            tg = self.dma(gst[:, :], dr["wgt"], f0)
            to = self.dma(ost[:, :, :], dr["wo_f"].rearrange("(k p) d -> p k d", p=128), f0)
            tb = self.dma(bo[:, :], bass.AP(dr["bo_f"].tensor, 0, [[0, 128], [1, 128]]), f0)
            t_w = self.split(Wh[:, :, :], Wl[:, :, :], wst[:, :, :], tw, f0)
            t_g = self.split(gh[:, :], gl[:, :], gst[:, :], tg)
            t_o = self.split(oh[:, :, :], ol[:, :, :], ost[:, :, :], to)
            z = DV.op(lambda e: e.memset(wst[:, :, :], 0.0), t_w)
            b1 = bass.AP(dr["b1"].tensor, 0, [[0, 2], [1, E * 512]])
            t = self.dma(wst[0:2, :, :].rearrange("p e h -> p (e h)"), b1, z)
            t = AC.op(lambda e: e.activation(bs[:, :, :], wst[:, :, :], ACT.Copy), t)
            t_b = DV.op(lambda e: e.scalar_tensor_tensor(
                bs[0:2, :, :].rearrange("p e h -> p (e h)"), bs[0:2, :, :].rearrange("p e h -> p (e h)").bitcast(F32),
                self.negrow[0:2, 0:1], wst[0:2, :, :].rearrange("p e h -> p (e h)"), ALU.mult, ALU.add), t, self.t_neg)

            t_xn = self.layernorm(c, xh, xl, lambda n: f0)

            lb = ps[:, 2, 0:NT * E].rearrange("p (n e) -> p n e", e=E)

            def logits(e):
                for n in range(NT):
                    cs = slice(128 * n, 128 * n + 128)
                    i = self.mm3(e, lb[:, n, :], xh[:, cs], xl[:, cs], gh[:, :], gl[:, :])
                return i
            p = PE.op(logits, t_g, *t_xn, f0)
            t = DV.op(lambda e: e.tensor_copy(lg[:, :, :], lb), p)
            for n in range(NT):
                t1 = DV.op(lambda e, n=n: e.max(v8[:, n, :], lg[:, n, :]), t)
            for n in range(NT):
                t2 = DV.op(lambda e, n=n: e.max_index(i8[:, n, :], v8[:, n, :], lg[:, n, :]), t1)
            top = bass.AP(v8[:, 0, 0:1].tensor, v8[:, 0, 0:1].offset, [v8[:, 0, :].ap[0], [8, NT], [0, E]])
            a = DV.op(lambda e: e.tensor_tensor(ex[:, :, :], lg[:, :, :], top, ALU.subtract), t2)
            a = AC.op(lambda e: e.activation(ex[:, :, :], ex[:, :, :], ACT.Exp), a)
            b = DV.op(lambda e: e.tensor_tensor(pv[:, :, :], v8[:, :, 0:2], bass.AP(top.tensor, top.offset,
                      [top.ap[0], [8, NT], [0, 2]]), ALU.subtract), t1)
            b = AC.op(lambda e: e.activation(pv[:, :, :], pv[:, :, :], ACT.Exp), b)
            t = DV.op(lambda e: e.reduce_sum(sm[:, :], ex[:, :, :], axis=AX), a)
            t = DV.op(lambda e: e.reciprocal(sm[:, :], sm[:, :]), t)

            def bc(v, n):
                y = v[:, :]
                return bass.AP(y.tensor, y.offset, [y.ap[0], [1, NT], [0, n]])
            t = DV.op(lambda e: e.tensor_tensor(pv[:, :, :], pv[:, :, :], bc(sm, 2), ALU.mult), t, b)
            t = DV.op(lambda e: e.tensor_tensor(den[:, :], pv[:, :, 0], pv[:, :, 1], ALU.add), t)
            t = DV.op(lambda e: e.tensor_scalar(den[:, :], den[:, :], EPS_TOPK, None, ALU.add), t)
            t = DV.op(lambda e: e.reciprocal(den[:, :], den[:, :]), t)
            t = DV.op(lambda e: e.tensor_tensor(pv[:, :, :], pv[:, :, :], bc(den, 2), ALU.mult), t)
            u = DV.op(lambda e: e.tensor_copy(if8[:, :, :], i8[:, :, 0:2]), t2)
            io = self.iota[:, :]
            iob = bass.AP(io.tensor, io.offset, [io.ap[0], [0, NT], [1, E]])
            for k, dst in ((0, comb), (1, oht)):
                ik = if8[:, :, k]
                ib = bass.AP(ik.tensor, ik.offset, [ik.ap[0], [2, NT], [0, E]])
                vk = pv[:, :, k]
                vb = bass.AP(vk.tensor, vk.offset, [vk.ap[0], [2, NT], [0, E]])
                w = DV.op(lambda e, ib=ib, dst=dst: e.tensor_tensor(dst[:, :, :], iob, ib, ALU.is_equal), u, self.t_const)
                t = DV.op(lambda e, vb=vb, dst=dst: e.tensor_tensor(dst[:, :, :], dst[:, :, :], vb, ALU.mult), w, t)
            t = DV.op(lambda e: e.tensor_tensor(comb[:, :, :], comb[:, :, :], oht[:, :, :], ALU.add), t)
            t_c = DV.op(lambda e: e.reduce_sum(csum[:, :], comb[:, :, :], axis=AX), t)

            hb_free = [None] * 4
            sig_free, acc_t = [None] * 4, {}
            gt_t, tr_free, y_free = [None, None], [None, None], [None, None]
            th_free = [None, None]
            pend = []

            def finish(n):
                s = n % 2
                bank = 4 + s

                def tr(e):
                    for k in range(2):
                        i = e.transpose(ps[:, bank, 128 * k:128 * k + 128], acc[:, s, 128 * k:128 * k + 128], self.ident[:, :])
                    return i
                p = PE.op(tr, acc_t[n], tr_free[s])
                r = self.split(th[:, s, :], tl[:, s, :], ps[:, bank, 0:256], p, th_free[s])
                tr_free[s] = r[1]
                acc_t[n] = p
                return s, r

            def project(n, s, r):
                yb = ps[:, 6 + s, 0:128]

                def emit(e):
                    for k in range(2):
                        cs = slice(128 * k, 128 * k + 128)
                        e.matmul(yb, th[:, s, cs], oh[:, k, :], start=k == 0, stop=False)
                        e.matmul(yb, th[:, s, cs], ol[:, k, :], start=False, stop=False)
                        i = e.matmul(yb, tl[:, s, cs], oh[:, k, :], start=False, stop=k == 1)
                    return i
                p = PE.op(emit, r, t_o, y_free[s])
                th_free[s] = p
                d = DV.op(lambda e: e.scalar_tensor_tensor(x[:, n, :], bo[:, :], csum[:, n:n + 1], x[:, n, :],
                          ALU.mult, ALU.add), tb, t_c, self.ln_end)
                y_free[s] = DV.op(lambda e: e.tensor_tensor(x[:, n, :], yb, x[:, n, :], ALU.add), d, p)

            units = [(n, k) for n in range(NT) for k in range(E)]
            fin = {}
            for i, (n, k) in enumerate(units):
                hb = ps[:, i % 4, :]
                cs = slice(128 * n, 128 * n + 128)

                def emit(e, hb=hb, cs=cs, k=k):
                    e.matmul(hb, xh[:, cs], Wh[:, k, :], start=True, stop=False)
                    e.matmul(hb, xh[:, cs], Wl[:, k, :], start=False, stop=False)
                    e.matmul(hb, xl[:, cs], Wh[:, k, :], start=False, stop=False)
                    return e.matmul(hb, self.ones[:, :], bs[:, k, :], start=False, stop=True)
                p = PE.op(emit, hb_free[i % 4], t_w, t_b, t_xn[n // 4], t_c if i < 4 else None, self.t_ones)
                a = AC.op(lambda e, i=i, hb=hb: e.activation(sig[:, i % 4, :], hb[:, FH:512], ACT.Sigmoid), p, sig_free[i % 4])
                s = n % 2
                if k == 0:
                    w = [acc_t.get(n - 2)]
                    d = DV.op(lambda e, i=i, hb=hb, n=n, s=s: e.scalar_tensor_tensor(
                        acc[:, s, :], hb[:, 0:FH], comb[:, n, 0:1], sig[:, i % 4, :], ALU.mult, ALU.mult), a, t_c, w)
                    acc_t[n] = d
                    hb_free[i % 4] = sig_free[i % 4] = d
                else:
                    d = DV.op(lambda e, i=i, hb=hb, n=n, k=k: e.scalar_tensor_tensor(
                        gt[:, k % 2, :], hb[:, 0:FH], comb[:, n, k:k + 1], sig[:, i % 4, :], ALU.mult, ALU.mult), a, gt_t[k % 2])
                    hb_free[i % 4] = sig_free[i % 4] = d
                    acc_t[n] = gt_t[k % 2] = DV.op(lambda e, k=k, s=s: e.tensor_tensor(
                        acc[:, s, :], acc[:, s, :], gt[:, k % 2, :], ALU.add), d, acc_t[n])
                if n and k == 1:
                    fin[n - 1] = finish(n - 1)
                if n and k == 4:
                    project(n - 1, *fin[n - 1])
            fin[NT - 1] = finish(NT - 1)
            project(NT - 1, *fin[NT - 1])

    def attention_b(self):
        nc, ps, x, dr = self.nc, self.ps, self.x, self.dr
        PE, AC, DV = self.pe, self.act, self.dve
        f0 = self.fence()
        c = ExitStack()
        with c:
            sb = lambda n, s, d: c.enter_context(nc.sbuf_tensor("b_" + n, s, d))
            xh, xl = sb("xh", [128, B * L], F32R), sb("xl", [128, B * L], F32R)
            wst = sb("wst", [128, 6, 128], F32)
            wvst = sb("wvst", [128, DB], F32)
            wh, wl = sb("wh", [128, 6, 128], F32R), sb("wl", [128, 6, 128], F32R)
            vh, vl = sb("vh", [128, DB], F32R), sb("vl", [128, DB], F32R)
            bq = sb("bq", [128, 6], F32)
            bvo = sb("bvo", [128, 136], F32)
            Q = sb("Q", [128, 4, L], F32R)
            y = sb("y", [128, 2, 512], F32)
            yh = sb("yh", [128, 2, 512], F32R)
            K = sb("K", [128, L], F32R)
            V = sb("V", [128, 8, 32], F32)
            mx = sb("mx", [128, 8, 4, 2], F32)
            m4 = sb("m4", [128, 8, 4], F32)
            m4h = sb("m4h", [128, 8, 4], F32R)
            NM = sb("NM", [128, 8, 4, 32], F32)
            P = sb("P", [128, 4, 2, 512], F32)
            os_ = sb("os", [128, 2, 512], F32)
            rl = sb("rl", [128, 2, 4, 4], F32)
            ao = sb("ao", [128, 8, 128], F32)
            ah, al = sb("ah", [128, 2, 512], F32R), sb("al", [128, 2, 512], F32R)

            tw = self.dma(wst[:, :, :], dr["w_b"].rearrange("d (k n) -> d k n", k=6), f0)
            tv = self.dma(wvst[:, :], dr["wv_b"], f0)
            tb = self.dma(bq[:, :], dr["bias_b"], f0)
            tb2 = self.dma(bvo[:, :], bass.AP(dr["bvo_b"].tensor, 0, [[0, 128], [1, 136]]), f0)
            t_w = self.split(wh[:, :, :], wl[:, :, :], wst[:, :, :], tw, f0)
            t_v = self.split(vh[:, :], vl[:, :], wvst[:, :], tv)
            t_nm0 = DV.op(lambda e: e.memset(NM[:, :, :, :], 0.0), f0)
            t_v0 = DV.op(lambda e: e.memset(V[:, :, :], 1.0), f0)
            t_m0 = DV.op(lambda e: e.memset(mx[:, :, :, :], NEG * 10), f0)
            t_xn = self.layernorm(c, xh, xl, lambda n: f0)
            pre = [t_w, t_v, tb, tb2, t_nm0, t_v0, t_m0]
            pre = [t for p in pre for t in (p if isinstance(p, list) else [p])]
            bov = bvo[:, 8:136]
            t_xb = DV.op(lambda e: e.tensor_tensor(x[:, :, :], x[:, :, :], bass.AP(
                bov.tensor, bov.offset, [bov.ap[0], [0, NT], [1, 128]]), ALU.add), tb2, self.ln_end)
            RS8 = 1.0 / math.sqrt(DB)

            XB = ps[:, 7, :]
            st = dict(x=None, o=None)
            mfree, sfree, pfree = [None, None], [None, None], [None] * 4
            yfree, osfree, ahfree = [None, None], [None, None], [None, None]
            nmx = [0]
            nst = [0]
            npr = [0]
            nyy = [0]
            prev_S = None
            prev_PV = None
            prev_tr = None
            ao_prev = None
            mx_prev, nm_prev = None, None

            for b in range(B):
                t_qk = []
                for g in range(5):
                    for half in range(2):
                        cs = slice(L * b + 512 * half, L * b + 512 * half + 512)
                        os = slice(512 * half, 512 * half + 512)
                        p = PE.op(lambda e, g=g, cs=cs: self.mm3(e, XB, wh[:, g, :], wl[:, g, :], xh[:, cs], xl[:, cs]),
                                  st["x"], pre, t_xn[2 * b + half], f0)
                        k = nyy[0] % 2
                        nyy[0] += 1
                        d = DV.op(lambda e, g=g, k=k: e.tensor_scalar(y[:, k, :], XB, bq[:, g:g + 1],
                                  RS8 if g < 4 else 1.0, ALU.add, ALU.mult), p, yfree[k])
                        st["x"] = d
                        a = AC.op(lambda e, k=k: e.activation(yh[:, k, :], y[:, k, :], ACT.Copy), d)
                        dst = Q[:, g, os] if g < 4 else K[:, os]
                        yfree[k] = DV.op(lambda e, k=k, dst=dst, g=g: e.scalar_tensor_tensor(
                            dst, yh[:, k, :].bitcast(F32), self.lowmask[:, (0 if g < 4 else 1):(1 if g < 4 else 2)],
                            y[:, k, :], ALU.mult, ALU.add), a, prev_S, self.t_low)
                        t_qk.append(yfree[k])

                def vmm(e, b=b):
                    for j in range(8):
                        cs = slice(L * b + 128 * j, L * b + 128 * j + 128)
                        i = self.mm3(e, ps[:, 7, 8 * j:8 * j + 8], xh[:, cs], xl[:, cs], vh[:, :], vl[:, :])
                    return i
                p = PE.op(vmm, st["x"], t_xn[2 * b], t_xn[2 * b + 1])
                bv = bvo[:, 0:8]
                t_V = DV.op(lambda e: e.tensor_tensor(V[:, :, 0:8], ps[:, 7, 0:64].rearrange("p (j d) -> p j d", d=8),
                            bass.AP(bv.tensor, bv.offset, [bv.ap[0], [0, 8], [1, 8]]), ALU.add), p, pre, prev_PV)
                st["x"] = t_V

                def maxima(g):
                    nonlocal mx_prev, nm_prev
                    for I in range(8):
                        for q in range(4):
                            for part in range(1 if I < 4 else 2):
                                k = nmx[0] % 2
                                nmx[0] += 1
                                w = min(512, 128 * (I + 1) - 512 * part)
                                diag = 128 * I // 512 == part

                                def emit(e, I=I, q=q, part=part, k=k, w=w, diag=diag):
                                    r = slice(32 * q, 32 * q + 32)
                                    i = e.matmul(ps[:, k, 0:w], Q[r, g, 128 * I:128 * I + 128],
                                                 K[r, 512 * part:512 * part + w], start=True, stop=not diag)
                                    if diag:
                                        i = e.matmul(ps[:, k, w - 128:w], self.identb[:, :], self.maskq[:, :],
                                                     start=False, stop=True)
                                    return i
                                p = PE.op(emit, mfree[k], t_qk)
                                mfree[k] = DV.op(lambda e, I=I, q=q, part=part, k=k, w=w: e.reduce_max(
                                    mx[:, I, q, part:part + 1], ps[:, k, 0:w], axis=AX), p, mx_prev, t_m0)
                    t = DV.op(lambda e: e.tensor_tensor(m4[:, :, :], mx[:, :, :, 0], mx[:, :, :, 1], ALU.max), mfree)
                    mx_prev = t
                    th = DV.op(lambda e: e.tensor_scalar(m4h[:, :, :], m4[:, :, :], -1.0, None, ALU.mult), t)
                    t1 = DV.op(lambda e: e.tensor_copy(NM[:, :, :, 24], m4h[:, :, :].bitcast(F32)), th, nm_prev, t_nm0)
                    t2 = DV.op(lambda e: e.scalar_tensor_tensor(NM[:, :, :, 25], m4[:, :, :], -1.0, m4h[:, :, :].bitcast(F32),
                               ALU.mult, ALU.subtract), th)
                    r = []
                    for half in range(2):
                        def tr(e, half=half):
                            for k in range(4):
                                i = e.transpose(ps[:, 7, 128 * k:128 * k + 128],
                                                NM[:, 4 * half + k, :, :].rearrange("p q r -> p (q r)"), self.ident[:, :])
                            return i
                        p = PE.op(tr, t1, t2, st["x"])
                        nm_prev = p
                        os = slice(512 * half, 512 * half + 512)
                        st["x"] = DV.op(lambda e, os=os: e.tensor_tensor(Q[:, g, os], XB, Q[:, g, os].bitcast(F32), ALU.add), p)
                        r.append(st["x"])
                    return r

                def sums(g, t_q2):
                    nonlocal prev_S, prev_PV, prev_tr
                    for ch in range(2):
                        OB = ps[:, 6, :]
                        todo = []

                        def pvs(J, off, pts, ch=ch):
                            nonlocal prev_PV

                            def emit(e):
                                for q in range(4):
                                    pt, hh = pts[q // 2][0], q % 2
                                    i = e.matmul(ps[32 * q:32 * q + 32, 6, off:512], V[:, J, :],
                                                 P[:, pt, hh, off:512], start=J == 4 * ch + 3, stop=J == 0,
                                                 skip_group_check=True)
                                return i
                            p = PE.op(emit, pts[0][1], pts[1][1], t_V, st["o"] if J == 4 * ch + 3 else None)
                            for pt, _ in pts:
                                pfree[pt] = p
                            prev_PV = p
                        for J in range(4 * ch + 3, -1, -1):
                            off = max(0, 128 * (J - 4 * ch))
                            diag = J >= 4 * ch
                            pts = []
                            for pr in range(2):
                                k = nst[0] % 2
                                nst[0] += 1

                                def emit(e, k=k, pr=pr, J=J, off=off, diag=diag, ch=ch):
                                    for hh in range(2):
                                        q = 2 * pr + hh
                                        r = slice(32 * q, 32 * q + 32)
                                        i = e.matmul(ps[:, 2 + 2 * k + hh, off:512], K[r, 128 * J:128 * J + 128],
                                                     Q[r, g, 512 * ch + off:512 * ch + 512], start=True, stop=not diag)
                                    if diag:
                                        for hh in range(2):
                                            i = e.matmul(ps[:, 2 + 2 * k + hh, off:off + 128], self.identb[:, :],
                                                         self.maskk[:, :], start=False, stop=True)
                                    return i
                                p = PE.op(emit, sfree[k], t_q2, t_qk)
                                prev_S = p
                                pt = npr[0] % 4
                                npr[0] += 1
                                sfree[k] = AC.op(lambda e, k=k, pt=pt, off=off: e.activation(
                                    P[:, pt, :, off:512], ps[:, 2 + 2 * k:4 + 2 * k, off:512], ACT.Exp), p, pfree[pt])
                                pts.append((pt, sfree[k]))
                            todo.append((J, off, pts))
                            if len(todo) > 1:
                                pvs(*todo.pop(0))
                        pvs(*todo.pop(0))
                        k = ch
                        a = AC.op(lambda e, k=k: e.activation(os_[:, k, :], ps[:, 6, :], ACT.Copy), prev_PV, osfree[k])
                        st["o"] = a

                        def tr(e, k=k):
                            for t in range(4):
                                i = e.transpose(ps[:, 7, 128 * t:128 * t + 128], os_[:, k, 128 * t:128 * t + 128], self.ident[:, :])
                            return i
                        osfree[k] = PE.op(tr, a, st["x"])
                        v = ps[:, 7, :].rearrange("p (t q r) -> p t q r", t=4, q=4)
                        d = DV.op(lambda e, k=k: e.reciprocal(rl[:, k, :, :], v[:, :, :, 8]), osfree[k])
                        rk = rl[:, k, :, :]
                        rb = bass.AP(rk.tensor, rk.offset, [rk.ap[0], [4, 4], [1, 4], [0, 8]])
                        dst = ao[:, 4 * ch:4 * ch + 4, 32 * g:32 * g + 32].rearrange("p t (q d) -> p t q d", q=4)
                        st["x"] = DV.op(lambda e, dst=dst, rb=rb: e.tensor_tensor(dst, v[:, :, :, 0:8], rb, ALU.mult), d, ao_prev)

                tq = maxima(0)
                for g in range(4):
                    tn = maxima(g + 1) if g < 3 else None
                    sums(g, tq)
                    tq = tn
                for half in range(2):
                    def tr(e, half=half):
                        for k in range(4):
                            i = e.transpose(ps[:, 7, 128 * k:128 * k + 128], ao[:, 4 * half + k, :], self.ident[:, :])
                        return i
                    p = PE.op(tr, st["x"])
                    ao_prev = p
                    r = self.split(ah[:, half, :], al[:, half, :], XB, p, ahfree[half])

                    def emit(e, half=half):
                        for k in range(4):
                            cs = slice(128 * k, 128 * k + 128)
                            i = self.mm3(e, ps[:, 7, cs], ah[:, half, cs], al[:, half, cs], wh[:, 5, :], wl[:, 5, :])
                        return i
                    p = PE.op(emit, r)
                    ahfree[half] = p
                    n0 = 8 * b + 4 * half
                    st["x"] = DV.op(lambda e, n0=n0: e.tensor_tensor(
                        x[:, n0:n0 + 4, :], XB.rearrange("p (k d) -> p k d", k=4), x[:, n0:n0 + 4, :], ALU.add), p, t_xb)

def build(nc, dram):
    p = Program(nc, dram)
    p.build()


def log_gamma(x):
    f = np.float32
    co = [676.520368121885098567009190444019, -1259.13921672240287047156078755283, 771.3234287776530788486528258894,
          -176.61502916214059906584551354, 12.507343278686904814458936853, -0.13857109526572011689554707,
          9.984369578019570859563e-6, 1.50563273514931155834e-7]
    z = (x - f(1)).astype(f)
    s = np.full_like(x, f(0.99999999999980993227684700473478))
    for i, c in enumerate(co):
        s = (s + f(c) / (z + f(i + 1))).astype(f)
    t = (f(7.5) + z).astype(f)
    lt = (f(math.log(7.5)) + np.log1p((z / f(7.5)).astype(f))).astype(f)
    return (((z + f(.5) - t / lt) * lt).astype(f) + (f(math.log(math.sqrt(2 * math.pi))) + np.log(s)).astype(f)).astype(f)


def features():
    f, n = np.float32, NF // 3
    d = np.arange(0, L, dtype=f)[:, None]
    half_life = (f(2.0) ** np.linspace(3.0, math.log(L) / math.log(2.0), n).astype(f)).astype(f)
    fe = np.exp((f(-math.log(2.0)) / half_life[None, :] * d).astype(f))
    cw = (f(2.0) ** np.arange(1, n + 1, dtype=f) - f(1.0)).astype(f)
    fc = (cw[None, :] > d).astype(f)
    std = L / (2.0 * n)
    mean = np.linspace(L / n, float(L), n).astype(f)[None, :]
    conc, rate = ((mean / f(std)) ** 2).astype(f), (mean / f(std ** 2)).astype(f)
    lu = ((conc - f(1)) * np.log(np.maximum(d, f(1))) - rate * d).astype(f)
    lu[0] = -np.inf
    ln = (log_gamma(conc) - (conc * np.log(rate)).astype(f)).astype(f)
    pr = (np.exp((lu - ln).astype(f)) + f(1e-8)).astype(f)
    return np.concatenate([fe, fc, pr / pr.max(-1, keepdims=True)], -1).astype(f)


def kernel(**inputs):
    import concourse.bacc as bacc
    from concourse.bass_utils import run_bass_kernel_spmd

    g = {k.replace("L0_", ""): np.asarray(v) for k, v in inputs.items()}
    feat = features()
    ft = np.zeros((NF, 2 * L), np.float32)
    ft[:, 0:2 * L - 1] = feat[np.abs(np.arange(2 * L - 1) - (L - 1))].T
    f0 = np.zeros((NF, 2), np.float32)
    f0[:, 1] = feat[0]

    def rows(w):
        a = np.zeros(w.shape[:-1] + (32,), w.dtype)
        for k in range(3):
            a[..., 8 * k:8 * k + 8] = w
        return a
    wq = rows(g["attn_b_Wq"].reshape(D, HB, DB)).reshape(D, 512)
    wk = rows(np.repeat(g["attn_b_Wk"][:, None, :], 4, 1)).reshape(D, 128)
    w_b = np.concatenate([wq, wk, g["attn_b_Wo"]], 1)
    bq = rows(g["attn_b_bq"].reshape(HB, DB)).reshape(4, 128)
    bk = rows(np.repeat(g["attn_b_bk"][None], 4, 0))
    bk[:, 24:26] = 1.0
    bias_b = np.concatenate([bq, bk.reshape(1, 128), np.zeros((1, 128), np.float32)], 0).T
    low = np.zeros((128, 2), np.float32)
    for q in range(4):
        low[32 * q + 8:32 * q + 16, 0] = -1.0
        low[32 * q + 16:32 * q + 24, 1] = -1.0
    arrays = {
        "q": g["attn_a_q"].reshape(B * L, D),
        "w_qs": g["attn_a_w_qs"], "w_ks": g["attn_a_w_ks"], "w_vs": g["attn_a_w_vs"],
        "w_rel": g["attn_a_w_rel_pos_k"], "w_out": g["attn_a_w_out"], "bo_a": g["attn_a_b_out"],
        "bias_a": np.concatenate([g["attn_a_rel_embed_bias"].reshape(H, DK), g["attn_a_rel_pos_bias"].reshape(H, DK)], 0).T,
        "feat": ft, "feat0": f0,
        "w_b": w_b, "wv_b": g["attn_b_Wv"], "bias_b": bias_b,
        "bvo_b": np.concatenate([g["attn_b_bv"], g["attn_b_bo"]]), "low": low,
        "wgt": g["ffn_Wg"].T, "w1t": g["ffn_W1"].transpose(2, 0, 1).reshape(D, E * 512),
        "b1": g["ffn_b1"].reshape(-1), "wo_f": g["ffn_Wo"].T, "bo_f": g["ffn_bo"],
    }
    nc = bacc.Bacc("TRN2", target_bir_lowering=False, num_devices=1, dynamic_dma_scratch_size=1024)
    arrays = {k: np.ascontiguousarray(v) for k, v in arrays.items()}
    dram = {k: nc.dram_tensor(f"in_{k}", v.shape, mybir.dt.from_np(v.dtype), kind="ExternalInput").ap()
            for k, v in arrays.items()}
    dram["out"] = nc.dram_tensor("out_0", (B * L, D), F32, kind="ExternalOutput").ap()
    build(nc, dram)
    r = run_bass_kernel_spmd(nc, [{f"in_{k}": v for k, v in arrays.items()}], core_ids=[0])
    return np.asarray(r.results[0]["out_0"]).reshape(B, L, D)
```

```python
import math
from contextlib import ExitStack

import numpy as np
import concourse.bass as bass
from concourse import mybir
from concourse.alu_op_type import AluOpType as ALU

F32 = mybir.dt.float32
F32R = mybir.dt.float32r
BF16 = mybir.dt.bfloat16
U32 = mybir.dt.uint32
ACT = mybir.ActivationFunctionType
AX = mybir.AxisListType.X

B, L, D = 4, 1024, 128
NT = B * L // 128
H, DK = 8, 128
NF = 96
E, FH = 8, 256
HB, DB = 16, 8
EPS_LN = 1e-5
EPS_TOPK = 1e-9
RW = 1152
NSP = 10
NEG = -1e30


class Token:

    def __init__(self, sem=None, value=None):
        self.sem, self.value, self.used = sem, value, sem is not None


class Queue:

    def __init__(self, sem):
        self.sem, self.items = sem, []

    def op(self, emit, *waits):
        flat = []
        for w in waits:
            flat += w if isinstance(w, (list, tuple)) else [w]
        flat = [w for w in flat if w is not None]
        for w in flat:
            w.used = True
        t = Token()
        self.items.append((flat, emit, t))
        return t

    def last(self):
        return [i[2] for i in self.items[-1:]]

    def number(self):
        n = 0
        for _, _, t in self.items:
            if t.sem is None and t.used:
                n += 1
                t.sem, t.value = self.sem, n

    def play(self, eng):
        seen = {}
        for waits, emit, t in self.items:
            need = {}
            for w in waits:
                if w.value > seen.get(w.sem.name, (None, 0))[1]:
                    if w.value > need.get(w.sem.name, (None, 0))[1]:
                        need[w.sem.name] = (w.sem, w.value)
            for name, (s, v) in need.items():
                eng.wait_ge(s, v)
                seen[name] = (s, v)
            ins = emit(eng)
            if t.sem is self.sem and t.used:
                ins.then_inc(self.sem, 1)


class DmaSem:

    def __init__(self, sem):
        self.sem, self.value = sem, 0

    def start(self, queue, out, in_, *waits):
        self.value += 16
        t = Token(self.sem, self.value)
        queue.op(lambda e: e.dma_start(out, in_).then_inc(self.sem, 16), *waits)
        return t


class Program:
    def __init__(self, nc, dram):
        self.nc, self.dr = nc, dram
        self.ctx = ExitStack()

    def sem(self, name):
        return self.ctx.enter_context(self.nc.semaphore(name))

    def fence(self):
        t = []
        for q in (self.pe, self.act, self.dve, self.pool):
            t += q.last()
        return t + self.dma_tokens

    def dma(self, out, in_, *waits, sem=None):
        if sem is None:
            sem = DmaSem(self.sem(f"dma{self.ndma}"))
            self.ndma += 1
        t = sem.start(self.sp, out, in_, *waits)
        return t

    def build(self):
        nc = self.nc
        with self.ctx:
            self.pe, self.act, self.dve, self.pool, self.sp = (
                Queue(self.sem("s_" + n)) for n in ("pe", "act", "dve", "pool", "sp"))
            self.ndma, self.dma_tokens = 0, []
            keep = self.ctx
            self.ps = keep.enter_context(nc.psum_tensor("ps", [128, 8, 512], F32))
            self.x = keep.enter_context(nc.sbuf_tensor("x", [128, NT, 128], F32))
            self.ident = keep.enter_context(nc.sbuf_tensor("ident", [128, 128], F32))
            self.identb = keep.enter_context(nc.sbuf_tensor("identb", [128, 128], BF16))
            self.maskq = keep.enter_context(nc.sbuf_tensor("maskq", [128, 128], BF16))
            self.maskk = keep.enter_context(nc.sbuf_tensor("maskk", [128, 128], BF16))
            self.ones = keep.enter_context(nc.sbuf_tensor("ones", [128, 128], F32R))
            self.iota = keep.enter_context(nc.sbuf_tensor("iota", [128, E], F32))
            self.negrow = keep.enter_context(nc.sbuf_tensor("negrow", [128, 1], F32))
            self.lowmask = keep.enter_context(nc.sbuf_tensor("lowmask", [128, 2], F32))
            self.constants()
            xin = self.dr["q"].rearrange("(n p) d -> p n d", p=128)
            self.t_x = [self.dma(self.x[:, 8 * b:8 * b + 8, :], xin[:, 8 * b:8 * b + 8, :]) for b in range(B)]
            xo = self.dr["out"].rearrange("(n p) d -> p n d", p=128)

            self.attention_a()
            self.ffn()
            self.attention_b()
            self.ffn()
            s_out = DmaSem(self.sem("s_out"))
            f = self.fence()
            t = s_out.start(self.sp, xo, self.x[:, :, :], f)
            self.sp.op(lambda e: e.wait_ge(t.sem, t.value))

            for q in (self.pe, self.act, self.dve, self.pool, self.sp):
                q.number()
            block = self.ctx.enter_context(nc.Block())
            block.sync(lambda e: self.sp.play(e))
            block.tensor(lambda e: self.pe.play(e))
            block.scalar(lambda e: self.act.play(e))
            block.vector(lambda e: self.dve.play(e))
            block.gpsimd(lambda e: self.pool.play(e))

    def constants(self):
        p = self.pool
        cond = dict(pattern=[[-1, 128]], channel_multiplier=1, base=0)
        a = p.op(lambda e: e.memset(self.ident[:, :], 0.0))
        b = p.op(lambda e: e.memset(self.identb[:, :], 0.0))
        c = p.op(lambda e: e.memset(self.maskq[:, :], 0.0))
        d = p.op(lambda e: e.memset(self.maskk[:, :], 0.0))
        self.t_ident = p.op(lambda e: e.affine_select(out=self.ident[:, :], in_=self.ident[:, :],
                            compare_op=ALU.not_equal, fill=1.0, **cond), a)
        p.op(lambda e: e.affine_select(out=self.identb[:, :], in_=self.identb[:, :],
             compare_op=ALU.not_equal, fill=1.0, **cond), b)
        p.op(lambda e: e.affine_select(out=self.maskq[:, :], in_=self.maskq[:, :],
             compare_op=ALU.is_ge, fill=NEG, **cond), c)
        p.op(lambda e: e.affine_select(out=self.maskk[:, :], in_=self.maskk[:, :], compare_op=ALU.is_ge,
             fill=NEG, pattern=[[1, 128]], channel_multiplier=-1, base=0), d)
        a = p.op(lambda e: e.memset(self.negrow[:, :], 0.0))
        self.t_neg = p.op(lambda e: e.affine_select(out=self.negrow[:, :], in_=self.negrow[:, :],
                          compare_op=ALU.not_equal, fill=-1.0, base=-1, pattern=[[0, 1]], channel_multiplier=1), a)
        a = self.dve.op(lambda e: e.memset(self.ones[:, :].bitcast(F32), 0.0))
        self.t_ones = self.dve.op(lambda e: e.memset(self.ones[0:2, :].bitcast(F32), 1.0), a)
        self.t_low = self.dma(self.lowmask[:, :], self.dr["low"])
        self.t_const = p.op(lambda e: e.iota(self.iota[:, :], pattern=[[1, E]], base=0, channel_multiplier=0,
                                             allow_small_or_imprecise_dtypes=True))

    def split(self, hi, lo, src, *waits, eng=None):
        a = self.act.op(lambda e: e.activation(hi, src, ACT.Copy), *waits)
        b = self.dve.op(lambda e: e.tensor_tensor(lo, src, hi.bitcast(F32), ALU.subtract), a)
        return [a, b]

    def mm3(self, e, out, lh, ll, rh, rl):
        e.matmul(out, lh, rh, start=True, stop=False)
        e.matmul(out, lh, rl, start=False, stop=False)
        return e.matmul(out, ll, rh, start=False, stop=True)

    def layernorm(self, ctx, xh, xl, start):
        nc, x = self.nc, self.x
        with ExitStack() as c:
            sb = lambda n, s, d: c.enter_context(nc.sbuf_tensor(f"ln{self.ndma}{n}", s, d))
            st = sb("st", [128, NT, 6], F32)
            mv = sb("mv", [128, NT, 2], F32)
            ve = sb("ve", [128, NT], F32)
            sd = sb("sd", [128, NT], F32)
            rs = sb("rs", [128, NT], F32)
            xn = sb("xn", [128, 4, 128], F32)
            self.ndma += 1
            for n in range(NT):
                t = self.dve.op(lambda e, n=n: e.bn_stats(st[:, n, :], x[:, n, :]), start(n))
            for n in range(NT):
                t2 = self.dve.op(lambda e, n=n: e.bn_aggr(mv[:, n, :], st[:, n, :]), t)
            t = self.dve.op(lambda e: e.tensor_scalar(ve[:, :], mv[:, :, 1], EPS_LN, None, ALU.add), t2)
            t = self.act.op(lambda e: e.activation(sd[:, :], ve[:, :], ACT.Sqrt), t)
            tr = self.dve.op(lambda e: e.reciprocal(rs[:, :], sd[:, :]), t)
            done, tp, lo = [], [None] * NT, [None, None]
            for n in range(NT):
                w = [tr] + ([tp[n - 4]] if n >= 4 else [])
                t = self.dve.op(lambda e, n=n: e.tensor_scalar(xn[:, n % 4, :], x[:, n, :], mv[:, n, 0:1],
                                rs[:, n:n + 1], ALU.subtract, ALU.mult), w)
                bank = (n // 4) % 2
                tp[n] = self.pe.op(lambda e, n=n, bank=bank: e.transpose(
                    self.ps[:, bank, 128 * (n % 4):128 * (n % 4) + 128], xn[:, n % 4, :], self.ident[:, :]),
                    t, lo[bank], self.t_ident, start(0))
                if n % 4 == 3:
                    cs = slice(128 * (n - 3), 128 * (n + 1))
                    hl = self.split(xh[:, cs], xl[:, cs], self.ps[:, bank, :], tp[n], start(0))
                    lo[bank] = hl[1]
                    done.append(hl)
            self.ln_end = self.dve.last() + self.act.last() + self.pe.last()
        return done

    def attention_a(self):
        nc, ps, x, dr = self.nc, self.ps, self.x, self.dr
        PE, AC, DV = self.pe, self.act, self.dve
        c = ExitStack()
        with c:
            sb = lambda n, s, d: c.enter_context(nc.sbuf_tensor("a_" + n, s, d))
            xh, xl = sb("xh", [128, B * L], F32R), sb("xl", [128, B * L], F32R)
            t_xn = self.layernorm(c, xh, xl, lambda n: self.t_x[n // 8])
            fh, fl = sb("fh", [NF, 2048], F32R), sb("fl", [NF, 2048], F32R)
            zh, zl = sb("zh", [NF, 2], F32R), sb("zl", [NF, 2], F32R)
            rh, rl = sb("rh", [128, 2048], F32R), sb("rl", [128, 2048], F32R)
            Kh, Kl = sb("Kh", [128, 2, L], F32R), sb("Kl", [128, 2, L], F32R)
            Vh, Vl = sb("Vh", [128, 2, L], F32R), sb("Vl", [128, 2, L], F32R)
            Qh, Ql = sb("Qh", [128, 2, 2, 512], F32R), sb("Ql", [128, 2, 2, 512], F32R)
            Ph, Pl = sb("Ph", [128, 4, 512], F32R), sb("Pl", [128, 4, 512], F32R)
            oh, ol = sb("oh", [128, 512], F32R), sb("ol", [128, 512], F32R)
            rt = sb("rt", [128, 2, RW], F32)
            sp = sb("sp", [128, NSP, L], F32)
            wst = sb("wst", [128, 4, 128], F32)
            wh, wl = sb("wh", [128, 2, 4, 128], F32R), sb("wl", [128, 2, 4, 128], F32R)
            gst = sb("gst", [NF, 2, 128], F32)
            gsm = sb("gsm", [NF, 3, 128], F32)
            gh, gl = sb("gh", [NF, 2, 3, 128], F32R), sb("gl", [NF, 2, 3, 128], F32R)
            bias = sb("bias", [128, 2, H], F32)
            nm = sb("nm", [128, 8], F32)
            ls = sb("ls", [128, 16], F32)
            rv = sb("rv", [128, 8], F32)
            bo = rt[:, 0, 0:128]
            scr = nc.dram_tensor("scr", (4, 128, RW), F32, kind="Internal").ap()

            lnw = self.ln_end
            t_bo = self.dma(bo, bass.AP(dr["bo_a"].tensor, 0, [[0, 128], [1, 128]]), lnw)
            t_bias = self.dma(bias[:, :, :], dr["bias_a"].rearrange("d (a h) -> d a h", a=2), lnw)
            t_xb = DV.op(lambda e: e.tensor_tensor(x[:, :, :], x[:, :, :], bass.AP(
                bo.tensor, bo.offset, [bo.ap[0], [0, NT], [1, 128]]), ALU.add), t_bo, lnw)
            fst = sp[0:NF, 0:2, :].rearrange("p a n -> p (a n)")
            t_f = self.dma(fst, dr["feat"], lnw)
            zst = sp[0:NF, 2, 0:2]
            t_z = self.dma(zst, dr["feat0"], lnw)
            t_fs = self.split(fh[:, :], fl[:, :], fst, t_f) + self.split(zh[:, :], zl[:, :], zst, t_z)

            s_w, s_g = DmaSem(self.sem("s_w")), DmaSem(self.sem("s_g"))
            s_wr = [DmaSem(self.sem(f"s_wr{i}")) for i in range(4)]
            s_rd = [DmaSem(self.sem(f"s_rd{i}")) for i in range(NSP)]

            SC = float(DK) ** -0.5
            NTI = H * NT
            t_wt, t_out = {}, {}
            st_free = [None]

            def weights(h):
                s = h % 2
                free = [st_free[0], t_out.get(4 * 2 * h - 9)]
                hs = slice(128 * h, 128 * h + 128)
                for k, nme in enumerate(("w_qs", "w_ks", "w_vs")):
                    tw = s_w.start(self.sp, wst[:, k, :], dr[nme][:, hs], *free, lnw)
                tw = s_w.start(self.sp, wst[:, 3, :], dr["w_out"][hs, :])
                tg = s_g.start(self.sp, gst[:, :, :], dr["w_rel"][:, hs].rearrange("(a p) n -> p a n", p=NF), *free, lnw)
                a = DV.op(lambda e: e.tensor_scalar(wst[:, 0, :], wst[:, 0, :], SC, None, ALU.mult), tw)
                b = [DV.op(lambda e: e.tensor_tensor(gsm[:, 0, :], gst[:, 0, :], gst[:, 1, :], ALU.subtract), tg, free),
                     DV.op(lambda e: e.tensor_tensor(gsm[:, 1, :], gst[:, 0, :], gst[:, 1, :], ALU.add)),
                     DV.op(lambda e: e.tensor_copy(gsm[:, 2, :], gst[:, 1, :]))]
                r = self.split(wh[:, s, :, :], wl[:, s, :, :], wst[:, :, :], a, free)
                r += self.split(gh[:, s, :, :], gl[:, s, :, :], gsm[:, :, :], b, free)
                st_free[0] = r[-1]
                t_wt[h] = r

            XB = ps[:, 7, :]
            OB = ps[:, 6, :]
            xfree = [None]
            rbank_free, tb_free, s_free, o_free = [None, None], [None, None], [None], [None]
            t_rel, t_q, t_k, t_v = [None] * 8, {}, {}, {}
            pe_R, pe_S, pe_T, pe_PV, pe_OUT = {}, {}, {}, {}, {}
            t_rd, t_wd, t_add, t_exp, t_PT, t_lo = {}, {}, {}, {}, {}, {}
            rev = {}

            def relunit(h, u):
                s, cs = h % 2, slice(256 * u, 256 * u + 256)
                g = 0 if u < 4 else 1
                out = ps[:, 7, 0:256]

                def emit(e):
                    i = self.mm3(e, out, gh[:, s, g, :], gl[:, s, g, :], fh[:, cs], fl[:, cs])
                    if u == 3:
                        i = self.mm3(e, ps[:, 7, 256:258], gh[:, s, 2, :], gl[:, s, 2, :], zh[:, :], zl[:, :])
                    return i
                p = PE.op(emit, xfree[0], t_wt[h], t_fs)
                last = pe_R.get(max(pe_R)) if pe_R else None
                if u == 3:
                    fix = DV.op(lambda e: e.tensor_copy(rv[:, 6:7], ps[:, 7, 257:258]), p)
                    p = DV.op(lambda e: e.tensor_tensor(ps[:, 7, 255:256], ps[:, 7, 255:256], rv[:, 6:7], ALU.add), fix)
                t_rel[u] = self.split(rh[:, cs], rl[:, cs], out, p, last)
                xfree[0] = t_rel[u][1]

            def qunit(qd):
                h, s = qd // 8, qd % 2
                cols = slice(512 * (qd % 8), 512 * (qd % 8) + 512)
                p = PE.op(lambda e: self.mm3(e, XB, wh[:, h % 2, 0, :], wl[:, h % 2, 0, :], xh[:, cols], xl[:, cols]),
                          xfree[0], t_wt[h], t_xn[qd % 8])
                war = [pe_S.get(4 * qd - 5), pe_R.get(4 * qd - 5)]
                a = [AC.op(lambda e, k=k: e.activation(Qh[:, s, k, :], XB, ACT.Identity, bias=bias[:, k, h:h + 1]),
                           p, war, t_bias) for k in range(2)]
                d = [DV.op(lambda e, k=k: e.scalar_tensor_tensor(Ql[:, s, k, :], XB, bias[:, k, h:h + 1],
                           Qh[:, s, k, :].bitcast(F32), ALU.add, ALU.subtract), a) for k in range(2)]
                t_q[qd] = a + d
                xfree[0] = d[1]

            def kunit(bh, half):
                h, b, s = bh // B, bh % B, bh % 2
                cols = slice(L * b + 512 * half, L * b + 512 * half + 512)
                p = PE.op(lambda e: self.mm3(e, XB, wh[:, h % 2, 1, :], wl[:, h % 2, 1, :], xh[:, cols], xl[:, cols]),
                          xfree[0], t_wt[h], t_xn[2 * b + half])
                o = slice(512 * half, 512 * half + 512)
                r = self.split(Kh[:, s, o], Kl[:, s, o], XB, p, pe_S.get(8 * (bh - 1) - 1))
                t_k.setdefault(bh, []).extend(r)
                xfree[0] = r[1]

            def vunit(bh, half):
                h, b, s = bh // B, bh % B, bh % 2

                def emit(e):
                    for j in range(4):
                        cs = slice(L * b + 512 * half + 128 * j, L * b + 512 * half + 128 * j + 128)
                        i = self.mm3(e, ps[:, 7, 128 * j:128 * j + 128], xh[:, cs], xl[:, cs],
                                     wh[:, h % 2, 2, :], wl[:, h % 2, 2, :])
                    return i
                p = PE.op(emit, xfree[0], t_wt[h], t_xn[2 * b + half])
                o = slice(512 * half, 512 * half + 512)
                r = self.split(Vh[:, s, o], Vl[:, s, o], XB, p, pe_PV.get((2 * (bh - 1) - 1, 7)))
                t_v[bh, half] = r
                xfree[0] = r[1]

            def rchunk(t, k):
                I, qd, s = t % 8, t // 4, (t // 4) % 2
                qs = slice(128 * (t % 4), 128 * (t % 4) + 128)
                rb = (3 * t + k) % 2
                cs = slice(896 - 128 * I + 384 * k, 896 - 128 * I + 384 * k + 384)
                units = [t_rel[u] for u in range(cs.start // 256, (cs.stop - 1) // 256 + 1)]
                pe_R[t] = PE.op(lambda e: self.mm3(e, ps[:, rb, 0:384], Qh[:, s, 1, qs], Ql[:, s, 1, qs],
                                rh[:, cs], rl[:, cs]), rbank_free[rb], t_q[qd], *units)
                rev.setdefault(t, []).append((pe_R[t], rt[:, t % 2, 384 * k:384 * k + 384], ps[:, rb, 0:384],
                                              [t_wd.get(t - 2), t_xb], rb))

            def revac(t, k):
                p, dst, src, war, rb = rev[t][k]
                if k == 1:
                    a = DV.op(lambda e: e.tensor_copy(dst, src), p, war)
                else:
                    a = AC.op(lambda e: e.activation(dst, src, ACT.Copy), p, war)
                rbank_free[rb] = a
                rev[t][k] = a

            def rwrite(t):
                t_wd[t] = s_wr[t % 4].start(self.sp, scr[t % 4, :, :], rt[:, t % 2, :], rev[t], t_rd.get(t - 4))

            def rread(t):
                src = bass.AP(scr.tensor, (t % 4) * 128 * RW + 127, [[RW - 1, 128], [1, L]])
                t_rd[t] = s_rd[t % NSP].start(self.sp, sp[:, t % NSP, :], src, t_wd[t], pe_T.get(((t - NSP) // 4, 7)), t_fs)

            def stile(t):
                bh, qd = t // 8, t // 4
                s, q2 = bh % 2, qd % 2
                qs = slice(128 * (t % 4), 128 * (t % 4) + 128)

                def emit(e):
                    for k in range(2):
                        cs = slice(512 * k, 512 * k + 512)
                        i = self.mm3(e, ps[:, 2 + k, :], Qh[:, q2, 0, qs], Ql[:, q2, 0, qs], Kh[:, s, cs], Kl[:, s, cs])
                    return i
                pe_S[t] = PE.op(emit, s_free[0], t_q[qd], t_k[bh])
                w = sp[:, t % NSP, :]
                t_add[t] = DV.op(lambda e: e.tensor_tensor_reduce(
                    out=w, in0=ps[:, 2:4, :].rearrange("p a n -> p (a n)"), in1=w, scale=-1.0, scalar=3e38,
                    op0=ALU.add, op1=ALU.min, accum_out=nm[:, t % 8:t % 8 + 1]), pe_S[t], t_rd[t], t_exp.get(t - 8))
                s_free[0] = t_add[t]

            def softmax(t):
                w = sp[:, t % NSP, :]
                t_exp[t] = AC.op(lambda e: e.activation(w, w, ACT.Exp, bias=nm[:, t % 8:t % 8 + 1], scale=-1.0,
                                 accum_out=ls[:, t % 16:t % 16 + 1]), t_add[t], t_out.get(t // 4 - 4))

            def tblock(qd, j):
                bank, slot = 4 + j % 2, j % 4

                def emit(e):
                    for k in range(4):
                        i = e.transpose(ps[:, bank, 128 * k:128 * k + 128],
                                        sp[:, (4 * qd + k) % NSP, 128 * j:128 * j + 128], self.ident[:, :])
                    return i
                p = PE.op(emit, *[t_exp[4 * qd + k] for k in range(4)], tb_free[j % 2])
                pe_T[qd, j] = p
                a = AC.op(lambda e: e.activation(Ph[:, slot, :], ps[:, bank, :], ACT.Copy), p,
                          pe_PV.get((qd, j - 4) if j > 3 else (qd - 1, j + 4)))
                t_PT[qd, j] = a

            def tlow(qd, j):
                bank, slot = 4 + j % 2, j % 4
                a = t_PT[qd, j]
                d = DV.op(lambda e: e.tensor_tensor(Pl[:, slot, :], ps[:, bank, :], Ph[:, slot, :].bitcast(F32),
                          ALU.subtract), a)
                tb_free[j % 2] = d
                t_PT[qd, j] = [a, d]

            def pv(qd, j):
                bh = qd // 2
                s, slot = bh % 2, j % 4
                cs = slice(128 * j, 128 * j + 128)

                def emit(e):
                    e.matmul(OB, Vh[:, s, cs], Ph[:, slot, :], start=j == 0, stop=False)
                    e.matmul(OB, Vh[:, s, cs], Pl[:, slot, :], start=False, stop=False)
                    return e.matmul(OB, Vl[:, s, cs], Ph[:, slot, :], start=False, stop=j == 7)
                pe_PV[qd, j] = PE.op(emit, t_PT[qd, j], t_v[bh, j // 4], o_free[0] if j == 0 else None)
                if j == 7:
                    t_lo[qd] = self.split(oh[:, :], ol[:, :], OB, pe_PV[qd, 7], pe_OUT.get(qd - 1))
                    o_free[0] = t_lo[qd][1]

            def outproj(qd):
                h = qd // 8

                def emit(e):
                    for k in range(4):
                        cs = slice(128 * k, 128 * k + 128)
                        i = self.mm3(e, ps[:, 7, cs], oh[:, cs], ol[:, cs], wh[:, h % 2, 3, :], wl[:, h % 2, 3, :])
                    return i
                pe_OUT[qd] = PE.op(emit, t_lo[qd], xfree[0], t_wt[h])
                c4 = (4 * qd) % 16
                r = DV.op(lambda e: e.reciprocal(rv[:, 0:4], ls[:, c4:c4 + 4]), t_exp[4 * qd + 3], t_out.get(qd - 1))
                for k in range(4):
                    n = 4 * (qd % 8) + k
                    t = DV.op(lambda e, k=k, n=n: e.scalar_tensor_tensor(
                        x[:, n, :], ps[:, 7, 128 * k:128 * k + 128], rv[:, k:k + 1], x[:, n, :], ALU.mult, ALU.add),
                        r, pe_OUT[qd], t_xb)
                t_out[qd] = t
                xfree[0] = t

            weights(0)
            for u in (7, 6, 5, 4, 3, 2, 1, 0):
                relunit(0, u)
            qunit(0)
            for half in range(2):
                kunit(0, half)
                vunit(0, half)
            for t in range(3):
                for k in range(3):
                    rchunk(t, k)
                    revac(t, k)
                rwrite(t)
                if t:
                    rread(t - 1)
            REL = {-1: (7,), 1: (6,), 3: (5,), 4: (4, 3), 6: (2,), 8: (1,), 10: (0,)}
            rel_at = {}
            for h in range(1, H):
                for ds, us in REL.items():
                    rel_at.setdefault(8 * (4 * h - 1) + ds, []).extend((h, u) for u in us)
            NQ = NTI // 4
            for s in range(NTI + 10):
                kq, qd, bh, p = s % 4, s // 4, s // 8, s // 4 - 1
                live, ahead, tlive = s < NTI, s + 3 < NTI, 0 <= p < NQ
                ja, jb = 2 * kq, 2 * kq + 1
                if live and s % 32 == 8 and s // 32 + 1 < H:
                    weights(s // 32 + 1)
                if live:
                    stile(s)
                if tlive:
                    tblock(p, ja)
                if kq == 0 and 0 < p <= NQ:
                    pv(p - 1, 7)
                if ahead:
                    rchunk(s + 3, 0)
                    revac(s + 3, 0)
                if live:
                    softmax(s)
                if tlive:
                    tlow(p, ja)
                if ahead:
                    rchunk(s + 3, 1)
                    revac(s + 3, 1)
                if kq and tlive:
                    pv(p, ja - 1)
                if kq == 0 and qd + 1 < NQ:
                    qunit(qd + 1)
                if kq == 1 and 0 < p <= NQ:
                    outproj(p - 1)
                if kq == 2 and live and bh + 1 < NTI // 8:
                    kunit(bh + 1, qd % 2)
                if kq == 3 and live:
                    if qd % 2 and bh + 1 < NTI // 8:
                        vunit(bh + 1, 0)
                    if qd % 2 == 0 and bh:
                        vunit(bh, 1)
                if tlive:
                    tblock(p, jb)
                if ahead:
                    rchunk(s + 3, 2)
                    revac(s + 3, 2)
                    rwrite(s + 3)
                if s + 2 < NTI:
                    rread(s + 2)
                if tlive:
                    tlow(p, jb)
                    pv(p, ja)
                for h, u in rel_at.get(s, ()):
                    relunit(h, u)
            self.dma_tokens = list(t_wd.values())[-4:] + list(t_rd.values())[-4:]

    def ffn(self):
        nc, ps, x, dr = self.nc, self.ps, self.x, self.dr
        PE, AC, DV = self.pe, self.act, self.dve
        f0 = self.fence()
        tag = f"f{self.ndma}_"
        c = ExitStack()
        with c:
            sb = lambda n, s, d: c.enter_context(nc.sbuf_tensor(tag + n, s, d))
            xh, xl = sb("xh", [128, B * L], F32R), sb("xl", [128, B * L], F32R)
            Wh, Wl = sb("Wh", [128, E, 512], F32R), sb("Wl", [128, E, 512], F32R)
            bs = sb("bs", [128, E, 512], F32R)
            wst = sb("wst", [128, E, 512], F32)
            gst = sb("gst", [128, E], F32)
            gh, gl = sb("gh", [128, E], F32R), sb("gl", [128, E], F32R)
            ost = sb("ost", [128, 2, 128], F32)
            oh, ol = sb("oh", [128, 2, 128], F32R), sb("ol", [128, 2, 128], F32R)
            bo = sb("bo", [128, 128], F32)
            lg = sb("lg", [128, NT, E], F32)
            ex = sb("ex", [128, NT, E], F32)
            v8 = sb("v8", [128, NT, 8], F32)
            i8 = sb("i8", [128, NT, 8], U32)
            if8 = sb("if8", [128, NT, 2], F32)
            sm = sb("sm", [128, NT], F32)
            pv = sb("pv", [128, NT, 2], F32)
            den = sb("den", [128, NT], F32)
            oht = sb("oht", [128, NT, E], F32)
            comb = sb("comb", [128, NT, E], F32)
            csum = sb("csum", [128, NT], F32)
            sig = sb("sig", [128, 4, FH], F32)
            gt = sb("gt", [128, 2, FH], F32)
            acc = sb("acc", [128, 2, FH], F32)
            th, tl = sb("th", [128, 2, FH], F32R), sb("tl", [128, 2, FH], F32R)

            tw = self.dma(wst[:, :, :], dr["w1t"].rearrange("d (e h) -> d e h", e=E), f0)
            tg = self.dma(gst[:, :], dr["wgt"], f0)
            to = self.dma(ost[:, :, :], dr["wo_f"].rearrange("(k p) d -> p k d", p=128), f0)
            tb = self.dma(bo[:, :], bass.AP(dr["bo_f"].tensor, 0, [[0, 128], [1, 128]]), f0)
            t_w = self.split(Wh[:, :, :], Wl[:, :, :], wst[:, :, :], tw, f0)
            t_g = self.split(gh[:, :], gl[:, :], gst[:, :], tg)
            t_o = self.split(oh[:, :, :], ol[:, :, :], ost[:, :, :], to)
            z = DV.op(lambda e: e.memset(wst[:, :, :], 0.0), t_w)
            b1 = bass.AP(dr["b1"].tensor, 0, [[0, 2], [1, E * 512]])
            t = self.dma(wst[0:2, :, :].rearrange("p e h -> p (e h)"), b1, z)
            t = AC.op(lambda e: e.activation(bs[:, :, :], wst[:, :, :], ACT.Copy), t)
            t_b = DV.op(lambda e: e.scalar_tensor_tensor(
                bs[0:2, :, :].rearrange("p e h -> p (e h)"), bs[0:2, :, :].rearrange("p e h -> p (e h)").bitcast(F32),
                self.negrow[0:2, 0:1], wst[0:2, :, :].rearrange("p e h -> p (e h)"), ALU.mult, ALU.add), t, self.t_neg)

            t_xn = self.layernorm(c, xh, xl, lambda n: f0)

            lb = ps[:, 2, 0:NT * E].rearrange("p (n e) -> p n e", e=E)

            def logits(e):
                for n in range(NT):
                    cs = slice(128 * n, 128 * n + 128)
                    i = self.mm3(e, lb[:, n, :], xh[:, cs], xl[:, cs], gh[:, :], gl[:, :])
                return i
            p = PE.op(logits, t_g, *t_xn, f0)
            t = DV.op(lambda e: e.tensor_copy(lg[:, :, :], lb), p)
            for n in range(NT):
                t1 = DV.op(lambda e, n=n: e.max(v8[:, n, :], lg[:, n, :]), t)
            for n in range(NT):
                t2 = DV.op(lambda e, n=n: e.max_index(i8[:, n, :], v8[:, n, :], lg[:, n, :]), t1)
            top = bass.AP(v8[:, 0, 0:1].tensor, v8[:, 0, 0:1].offset, [v8[:, 0, :].ap[0], [8, NT], [0, E]])
            a = DV.op(lambda e: e.tensor_tensor(ex[:, :, :], lg[:, :, :], top, ALU.subtract), t2)
            a = AC.op(lambda e: e.activation(ex[:, :, :], ex[:, :, :], ACT.Exp), a)
            b = DV.op(lambda e: e.tensor_tensor(pv[:, :, :], v8[:, :, 0:2], bass.AP(top.tensor, top.offset,
                      [top.ap[0], [8, NT], [0, 2]]), ALU.subtract), t1)
            b = AC.op(lambda e: e.activation(pv[:, :, :], pv[:, :, :], ACT.Exp), b)
            t = DV.op(lambda e: e.reduce_sum(sm[:, :], ex[:, :, :], axis=AX), a)
            t = DV.op(lambda e: e.reciprocal(sm[:, :], sm[:, :]), t)

            def bc(v, n):
                y = v[:, :]
                return bass.AP(y.tensor, y.offset, [y.ap[0], [1, NT], [0, n]])
            t = DV.op(lambda e: e.tensor_tensor(pv[:, :, :], pv[:, :, :], bc(sm, 2), ALU.mult), t, b)
            t = DV.op(lambda e: e.tensor_tensor(den[:, :], pv[:, :, 0], pv[:, :, 1], ALU.add), t)
            t = DV.op(lambda e: e.tensor_scalar(den[:, :], den[:, :], EPS_TOPK, None, ALU.add), t)
            t = DV.op(lambda e: e.reciprocal(den[:, :], den[:, :]), t)
            t = DV.op(lambda e: e.tensor_tensor(pv[:, :, :], pv[:, :, :], bc(den, 2), ALU.mult), t)
            u = DV.op(lambda e: e.tensor_copy(if8[:, :, :], i8[:, :, 0:2]), t2)
            io = self.iota[:, :]
            iob = bass.AP(io.tensor, io.offset, [io.ap[0], [0, NT], [1, E]])
            for k, dst in ((0, comb), (1, oht)):
                ik = if8[:, :, k]
                ib = bass.AP(ik.tensor, ik.offset, [ik.ap[0], [2, NT], [0, E]])
                vk = pv[:, :, k]
                vb = bass.AP(vk.tensor, vk.offset, [vk.ap[0], [2, NT], [0, E]])
                w = DV.op(lambda e, ib=ib, dst=dst: e.tensor_tensor(dst[:, :, :], iob, ib, ALU.is_equal), u, self.t_const)
                t = DV.op(lambda e, vb=vb, dst=dst: e.tensor_tensor(dst[:, :, :], dst[:, :, :], vb, ALU.mult), w, t)
            t = DV.op(lambda e: e.tensor_tensor(comb[:, :, :], comb[:, :, :], oht[:, :, :], ALU.add), t)
            t_c = DV.op(lambda e: e.reduce_sum(csum[:, :], comb[:, :, :], axis=AX), t)

            hb_free = [None] * 4
            sig_free, acc_t = [None] * 4, {}
            gt_t, tr_free, y_free = [None, None], [None, None], [None, None]
            th_free = [None, None]
            pend = []

            def finish(n):
                s = n % 2
                bank = 4 + s

                def tr(e):
                    for k in range(2):
                        i = e.transpose(ps[:, bank, 128 * k:128 * k + 128], acc[:, s, 128 * k:128 * k + 128], self.ident[:, :])
                    return i
                p = PE.op(tr, acc_t[n], tr_free[s])
                r = self.split(th[:, s, :], tl[:, s, :], ps[:, bank, 0:256], p, th_free[s])
                tr_free[s] = r[1]
                acc_t[n] = p
                return s, r

            def project(n, s, r):
                yb = ps[:, 6 + s, 0:128]

                def emit(e):
                    for k in range(2):
                        cs = slice(128 * k, 128 * k + 128)
                        e.matmul(yb, th[:, s, cs], oh[:, k, :], start=k == 0, stop=False)
                        e.matmul(yb, th[:, s, cs], ol[:, k, :], start=False, stop=False)
                        i = e.matmul(yb, tl[:, s, cs], oh[:, k, :], start=False, stop=k == 1)
                    return i
                p = PE.op(emit, r, t_o, y_free[s])
                th_free[s] = p
                d = DV.op(lambda e: e.scalar_tensor_tensor(x[:, n, :], bo[:, :], csum[:, n:n + 1], x[:, n, :],
                          ALU.mult, ALU.add), tb, t_c, self.ln_end)
                y_free[s] = DV.op(lambda e: e.tensor_tensor(x[:, n, :], yb, x[:, n, :], ALU.add), d, p)

            units = [(n, k) for n in range(NT) for k in range(E)]
            fin = {}
            for i, (n, k) in enumerate(units):
                hb = ps[:, i % 4, :]
                cs = slice(128 * n, 128 * n + 128)

                def emit(e, hb=hb, cs=cs, k=k):
                    e.matmul(hb, xh[:, cs], Wh[:, k, :], start=True, stop=False)
                    e.matmul(hb, xh[:, cs], Wl[:, k, :], start=False, stop=False)
                    e.matmul(hb, xl[:, cs], Wh[:, k, :], start=False, stop=False)
                    return e.matmul(hb, self.ones[:, :], bs[:, k, :], start=False, stop=True)
                p = PE.op(emit, hb_free[i % 4], t_w, t_b, t_xn[n // 4], t_c if i < 4 else None, self.t_ones)
                a = AC.op(lambda e, i=i, hb=hb: e.activation(sig[:, i % 4, :], hb[:, FH:512], ACT.Sigmoid), p, sig_free[i % 4])
                s = n % 2
                if k == 0:
                    w = [acc_t.get(n - 2)]
                    d = DV.op(lambda e, i=i, hb=hb, n=n, s=s: e.scalar_tensor_tensor(
                        acc[:, s, :], hb[:, 0:FH], comb[:, n, 0:1], sig[:, i % 4, :], ALU.mult, ALU.mult), a, t_c, w)
                    acc_t[n] = d
                    hb_free[i % 4] = sig_free[i % 4] = d
                else:
                    d = DV.op(lambda e, i=i, hb=hb, n=n, k=k: e.scalar_tensor_tensor(
                        gt[:, k % 2, :], hb[:, 0:FH], comb[:, n, k:k + 1], sig[:, i % 4, :], ALU.mult, ALU.mult), a, gt_t[k % 2])
                    hb_free[i % 4] = sig_free[i % 4] = d
                    acc_t[n] = gt_t[k % 2] = DV.op(lambda e, k=k, s=s: e.tensor_tensor(
                        acc[:, s, :], acc[:, s, :], gt[:, k % 2, :], ALU.add), d, acc_t[n])
                if n and k == 1:
                    fin[n - 1] = finish(n - 1)
                if n and k == 4:
                    project(n - 1, *fin[n - 1])
            fin[NT - 1] = finish(NT - 1)
            project(NT - 1, *fin[NT - 1])

    def attention_b(self):
        nc, ps, x, dr = self.nc, self.ps, self.x, self.dr
        PE, AC, DV = self.pe, self.act, self.dve
        f0 = self.fence()
        c = ExitStack()
        with c:
            sb = lambda n, s, d: c.enter_context(nc.sbuf_tensor("b_" + n, s, d))
            xh, xl = sb("xh", [128, B * L], F32R), sb("xl", [128, B * L], F32R)
            wst = sb("wst", [128, 6, 128], F32)
            wvst = sb("wvst", [128, DB], F32)
            wh, wl = sb("wh", [128, 6, 128], F32R), sb("wl", [128, 6, 128], F32R)
            vh, vl = sb("vh", [128, DB], F32R), sb("vl", [128, DB], F32R)
            bq = sb("bq", [128, 6], F32)
            bvo = sb("bvo", [128, 136], F32)
            Q = sb("Q", [128, 2, 4, L], F32R)
            y = sb("y", [128, 2, 512], F32)
            yh = sb("yh", [128, 2, 512], F32R)
            yk = sb("yk", [128, 2, 512], F32R)
            K = sb("K", [128, 2, 4, L], F32R)
            V = sb("V", [128, 2, 8, 32], F32)
            mx = sb("mx", [128, 8, 4, 2], F32)
            m4 = sb("m4", [128, 8, 4], F32)
            m4h = sb("m4h", [128, 8, 4], F32R)
            NM = sb("NM", [128, 8, 4, 32], F32)
            P = sb("P", [128, 8, 512], F32)
            os_ = sb("os", [128, 2, 512], F32)
            rl = sb("rl", [128, 2, 4, 4], F32)
            ao = sb("ao", [128, 2, 8, 128], F32)
            ah, al = sb("ah", [128, 2, 512], F32R), sb("al", [128, 2, 512], F32R)

            RS8 = 1.0 / math.sqrt(DB)
            tw = self.dma(wst[:, :, :], dr["w_b"].rearrange("d (k n) -> d k n", k=6), f0)
            tv = self.dma(wvst[:, :], dr["wv_b"], f0)
            tb = self.dma(bq[:, :], dr["bias_b"], f0)
            tb2 = self.dma(bvo[:, :], bass.AP(dr["bvo_b"].tensor, 0, [[0, 128], [1, 136]]), f0)
            t_w = self.split(wh[:, :, :], wl[:, :, :], wst[:, :, :], tw, f0)
            t_v = self.split(vh[:, :], vl[:, :], wvst[:, :], tv)
            t_nm0 = DV.op(lambda e: e.memset(NM[:, :, :, :], 0.0), f0)
            t_v0 = DV.op(lambda e: e.memset(V[:, :, :, :], 1.0), f0)
            t_bq = DV.op(lambda e: e.tensor_scalar(bq[:, 0:4], bq[:, 0:4], RS8, None, ALU.mult), tb)
            t_k0 = self.pool.op(lambda e: e.memset(K[:, :, :, :].bitcast(F32), 0.0), f0)
            t_m0 = DV.op(lambda e: e.memset(mx[:, :, :, :], NEG * 10), f0)
            t_xn = self.layernorm(c, xh, xl, lambda n: f0)
            pre = [t_w, t_v, t_bq, tb2, t_nm0, t_v0, t_m0]
            pre = [t for p in pre for t in (p if isinstance(p, list) else [p])]
            bov = bvo[:, 8:136]
            t_xb = DV.op(lambda e: e.tensor_tensor(x[:, :, :], x[:, :, :], bass.AP(
                bov.tensor, bov.offset, [bov.ap[0], [0, NT], [1, 128]]), ALU.add), tb2, self.ln_end)

            XB = ps[:, 7, :]
            st = dict(x=None, o=None)
            mfree, sfree, pfree = [None] * 3, [None] * 3, [None] * 8
            yfree, osfree, ahfree = [None, None], [None, None], [None, None]
            nmx = [0]
            nst = [0]
            npr = [0]
            nyy = [0]
            last_S, last_PV, last_AO = {}, {}, {}
            t_qk, t_q2, t_V, t_K = {}, {}, {}, {}
            hold = dict(mx=None, nm=None, pv=None)

            def proj(b, g, half):
                cs = slice(L * b + 512 * half, L * b + 512 * half + 512)
                os = slice(512 * half, 512 * half + 512)
                p = PE.op(lambda e: self.mm3(e, XB, wh[:, g, :], wl[:, g, :], xh[:, cs], xl[:, cs]),
                          st["x"], pre, t_xn[2 * b + half], f0)
                k = nyy[0] % 2
                nyy[0] += 1
                d = AC.op(lambda e: e.activation(y[:, k, :], XB, ACT.Identity, bias=bq[:, g:g + 1],
                          scale=RS8 if g < 4 else 1.0), p, yfree[k])
                st["x"] = d
                a = AC.op(lambda e: e.activation(yh[:, k, :], y[:, k, :], ACT.Copy), d)
                m = 0 if g < 4 else 1
                dst = Q[:, b % 2, g, os] if g < 4 else yk[:, half, :]
                yfree[k] = DV.op(lambda e: e.scalar_tensor_tensor(dst, yh[:, k, :].bitcast(F32), self.lowmask[:, m:m + 1],
                                 y[:, k, :], ALU.mult, ALU.add), a, last_S.get(b - 2) if g < 4 else t_K.get((b - 1, half)),
                                 self.t_low)
                t = [yfree[k]]
                if g == 4:
                    t = [self.pool.op(lambda e, q=q: e.tensor_copy(K[32 * q:32 * q + 32, b % 2, q, os],
                         yk[32 * q:32 * q + 32, half, :].bitcast(F32)), yfree[k], last_S.get(b - 2), t_k0) for q in range(4)]
                    t_K[b, half] = t[-1]
                t_qk.setdefault((b, g), []).extend(t[-1:])

            def values(b):
                def emit(e):
                    for j in range(8):
                        cs = slice(L * b + 128 * j, L * b + 128 * j + 128)
                        i = self.mm3(e, ps[:, 7, 8 * j:8 * j + 8], xh[:, cs], xl[:, cs], vh[:, :], vl[:, :])
                    return i
                p = PE.op(emit, st["x"], t_xn[2 * b], t_xn[2 * b + 1])
                bv = bvo[:, 0:8]
                t_V[b] = DV.op(lambda e: e.tensor_tensor(V[:, b % 2, :, 0:8], ps[:, 7, 0:64].rearrange("p (j d) -> p j d", d=8),
                               bass.AP(bv.tensor, bv.offset, [bv.ap[0], [0, 8], [1, 8]]), ALU.add), p, pre, last_PV.get(b - 2))
                st["x"] = t_V[b]

            def maximum(b, g, I, q, part):
                k = nmx[0] % 3
                nmx[0] += 1
                w = min(512, 128 * (I + 1) - 512 * part)
                diag = I // 4 == part

                def emit(e):
                    i = e.matmul(ps[:, k, 0:w], Q[:, b % 2, g, 128 * I:128 * I + 128],
                                 K[:, b % 2, q, 512 * part:512 * part + w], start=True, stop=not diag)
                    if diag:
                        i = e.matmul(ps[:, k, w - 128:w], self.identb[:, :], self.maskq[:, :], start=False, stop=True)
                    return i
                p = PE.op(emit, mfree[k], t_qk[b, g], t_qk[b, 4])
                mfree[k] = DV.op(lambda e: e.reduce_max(mx[:, I, q, part:part + 1], ps[:, k, 0:w], axis=AX),
                                 p, hold["mx"], t_m0)

            def shift(b, g):
                t = DV.op(lambda e: e.tensor_tensor(m4[:, :, :], mx[:, :, :, 0], mx[:, :, :, 1], ALU.max), mfree)
                hold["mx"] = t
                th = DV.op(lambda e: e.tensor_scalar(m4h[:, :, :], m4[:, :, :], -1.0, None, ALU.mult), t)
                t1 = DV.op(lambda e: e.tensor_copy(NM[:, :, :, 24], m4h[:, :, :].bitcast(F32)), th, hold["nm"], t_nm0)
                t2 = DV.op(lambda e: e.scalar_tensor_tensor(NM[:, :, :, 25], m4[:, :, :], -1.0, m4h[:, :, :].bitcast(F32),
                           ALU.mult, ALU.subtract), th)
                hold["t"] = [t1, t2]

            def shift2(b, g, half):
                def tr(e):
                    for k in range(4):
                        i = e.transpose(ps[:, 7, 128 * k:128 * k + 128],
                                        NM[:, 4 * half + k, :, :].rearrange("p q r -> p (q r)"), self.ident[:, :])
                    return i
                hold["nm"] = PE.op(tr, hold["t"], st["x"])
                os = slice(512 * half, 512 * half + 512)
                st["x"] = DV.op(lambda e: e.tensor_tensor(Q[:, b % 2, g, os], XB, Q[:, b % 2, g, os].bitcast(F32), ALU.add),
                                hold["nm"])
                t_q2.setdefault((b, g), []).append(st["x"])

            def scores(b, g, ch, J, q):
                off = max(0, 128 * (J - 4 * ch))
                diag = J >= 4 * ch
                k = 3 + nst[0] % 3
                pt = nst[0] % 8
                nst[0] += 1

                def emit(e):
                    i = e.matmul(ps[:, k, off:512], K[:, b % 2, q, 128 * J:128 * J + 128],
                                 Q[:, b % 2, g, 512 * ch + off:512 * ch + 512], start=True, stop=not diag)
                    if diag:
                        i = e.matmul(ps[:, k, off:off + 128], self.identb[:, :], self.maskk[:, :], start=False, stop=True)
                    return i
                p = PE.op(emit, sfree[k - 3], t_q2[b, g][ch])
                last_S[b] = p
                sfree[k - 3] = AC.op(lambda e: e.activation(P[:, pt, off:512], ps[:, k, off:512], ACT.Exp), p, pfree[pt])
                return pt, sfree[k - 3]

            def weighted(b, g, ch, J, pts):
                off = max(0, 128 * (J - 4 * ch))

                def emit(e):
                    for q in range(4):
                        i = e.matmul(ps[32 * q:32 * q + 32, 6, off:512], V[:, b % 2, J, :], P[:, pts[q][0], off:512],
                                     start=J == 4 * ch + 3, stop=J == 0, skip_group_check=True)
                    return i
                p = PE.op(emit, [t for _, t in pts], t_V[b], st["o"] if J == 4 * ch + 3 else None)
                for pt, _ in pts:
                    pfree[pt] = p
                hold["pv"] = last_PV[b] = p

            def normal1(b, g, ch):
                a = AC.op(lambda e: e.activation(os_[:, ch, :], ps[:, 6, :], ACT.Copy), hold["pv"], osfree[ch])
                st["o"] = a
                hold["os", ch] = a

            def normal2(b, g, ch):
                def tr(e):
                    for t in range(4):
                        i = e.transpose(ps[:, 7, 128 * t:128 * t + 128], os_[:, ch, 128 * t:128 * t + 128], self.ident[:, :])
                    return i
                osfree[ch] = PE.op(tr, hold["os", ch], st["x"])
                v = ps[:, 7, :].rearrange("p (t q r) -> p t q r", t=4, q=4)
                d = DV.op(lambda e: e.reciprocal(rl[:, ch, :, :], v[:, :, :, 8]), osfree[ch])
                rk = rl[:, ch, :, :]
                rb = bass.AP(rk.tensor, rk.offset, [rk.ap[0], [4, 4], [1, 4], [0, 8]])
                dst = ao[:, b % 2, 4 * ch:4 * ch + 4, 32 * g:32 * g + 32].rearrange("p t (q d) -> p t q d", q=4)
                st["x"] = DV.op(lambda e: e.tensor_tensor(dst, v[:, :, :, 0:8], rb, ALU.mult), d, last_AO.get(b - 2))
                hold["ao", b] = st["x"]

            def out1(b, half):
                def tr(e):
                    for k in range(4):
                        i = e.transpose(ps[:, 7, 128 * k:128 * k + 128], ao[:, b % 2, 4 * half + k, :], self.ident[:, :])
                    return i
                p = PE.op(tr, st["x"], hold["ao", b])
                last_AO[b] = p
                hold["oh", half] = self.split(ah[:, half, :], al[:, half, :], XB, p, ahfree[half])
                st["x"] = hold["oh", half][1]

            def out2(b, half):
                def emit(e):
                    for k in range(4):
                        cs = slice(128 * k, 128 * k + 128)
                        i = self.mm3(e, ps[:, 7, cs], ah[:, half, cs], al[:, half, cs], wh[:, 5, :], wl[:, 5, :])
                    return i
                p = PE.op(emit, hold["oh", half], st["x"])
                ahfree[half] = p
                n0 = 8 * b + 4 * half
                st["x"] = DV.op(lambda e: e.tensor_tensor(x[:, n0:n0 + 4, :], XB.rearrange("p (k d) -> p k d", k=4),
                                x[:, n0:n0 + 4, :], ALU.add), p, t_xb)

            def spread(many, few, start=0):
                r, at = list(many[:start]), 0
                rest = many[start:]
                for i, m in enumerate(rest):
                    r.append(m)
                    upto = len(few) * (i + 1) // len(rest)
                    r += few[at:upto]
                    at = upto
                return r

            def first(b):
                return [(proj, (b, k, half)) for k in (4, 0) for half in range(2)] + [(values, (b,))]

            def prepare(n):
                b, g = n // 4, n % 4
                m = [(maximum, (b, g, I, q, part)) for I in range(8) for q in range(4) for part in range(1 + I // 4)]
                p = [(proj, (b, g + 1, half)) for half in range(2)] if g < 3 else first(b + 1) if b + 1 < B else []
                return spread(m, p), [(shift, (b, g))] + [(shift2, (b, g, half)) for half in range(2)]

            def finish(n):
                b, g = n // 4, n % 4
                r, prev, pts = [], [], {}

                def sc(ch, J, q):
                    pts.setdefault((ch, J), []).append(scores(b, g, ch, J, q))
                for ch in range(2):
                    for J in range(4 * ch + 3, -1, -1):
                        r += [(sc, (ch, J, q)) for q in range(3)] + prev + [(sc, (ch, J, 3))]
                        prev = [(lambda ch, J: weighted(b, g, ch, J, pts[ch, J]), (ch, J))]
                        if J == 0:
                            prev.append((normal1, (b, g, ch)))
                return r, prev

            for f, a in first(0) + sum(prepare(0), []):
                f(*a)
            late, tail = [], []
            for n in range(16):
                b, g = n // 4, n % 4
                main, end = finish(n)
                main = main[:3] + tail + main[3:]
                tail = end
                k = next(i for i, (f, a) in enumerate(main) if f is normal1 and a == (b, g, 0))
                main.insert(k + 6, (normal2, (b, g, 0)))
                m, e = prepare(n + 1) if n < 15 else ([], [])
                side = spread(m, late, 4) if m else late
                late = [(normal2, (b, g, 1))]
                if g == 3:
                    late += [(o, (b, half)) for half in range(2) for o in (out1, out2)]
                stop = len(main) - 12
                at = 0
                for i, (f, a) in enumerate(main):
                    f(*a)
                    if i >= 4:
                        upto = min(len(side), -(-len(side) * (i - 3) // (stop - 4)))
                        for h, c2 in side[at:upto]:
                            h(*c2)
                        at = upto
                    if e and i >= stop and (i - stop) % 4 == 0:
                        h, c2 = e.pop(0)
                        h(*c2)
                for h, c2 in e:
                    h(*c2)
            for f, a in tail + late:
                f(*a)


def build(nc, dram):
    p = Program(nc, dram)
    p.build()


def log_gamma(x):
    f = np.float32
    co = [676.520368121885098567009190444019, -1259.13921672240287047156078755283, 771.3234287776530788486528258894,
          -176.61502916214059906584551354, 12.507343278686904814458936853, -0.13857109526572011689554707,
          9.984369578019570859563e-6, 1.50563273514931155834e-7]
    z = (x - f(1)).astype(f)
    s = np.full_like(x, f(0.99999999999980993227684700473478))
    for i, c in enumerate(co):
        s = (s + f(c) / (z + f(i + 1))).astype(f)
    t = (f(7.5) + z).astype(f)
    lt = (f(math.log(7.5)) + np.log1p((z / f(7.5)).astype(f))).astype(f)
    return (((z + f(.5) - t / lt) * lt).astype(f) + (f(math.log(math.sqrt(2 * math.pi))) + np.log(s)).astype(f)).astype(f)


def features():
    f, n = np.float32, NF // 3
    d = np.arange(0, L, dtype=f)[:, None]
    half_life = (f(2.0) ** np.linspace(3.0, math.log(L) / math.log(2.0), n).astype(f)).astype(f)
    fe = np.exp((f(-math.log(2.0)) / half_life[None, :] * d).astype(f))
    cw = (f(2.0) ** np.arange(1, n + 1, dtype=f) - f(1.0)).astype(f)
    fc = (cw[None, :] > d).astype(f)
    std = L / (2.0 * n)
    mean = np.linspace(L / n, float(L), n).astype(f)[None, :]
    conc, rate = ((mean / f(std)) ** 2).astype(f), (mean / f(std ** 2)).astype(f)
    lu = ((conc - f(1)) * np.log(np.maximum(d, f(1))) - rate * d).astype(f)
    lu[0] = -np.inf
    ln = (log_gamma(conc) - (conc * np.log(rate)).astype(f)).astype(f)
    pr = (np.exp((lu - ln).astype(f)) + f(1e-8)).astype(f)
    return np.concatenate([fe, fc, pr / pr.max(-1, keepdims=True)], -1).astype(f)


def kernel(**inputs):
    import concourse.bacc as bacc
    from concourse.bass_utils import run_bass_kernel_spmd

    g = {k.replace("L0_", ""): np.asarray(v) for k, v in inputs.items()}
    feat = features()
    ft = np.zeros((NF, 2 * L), np.float32)
    ft[:, 0:2 * L - 1] = feat[np.abs(np.arange(2 * L - 1) - (L - 1))].T
    f0 = np.zeros((NF, 2), np.float32)
    f0[:, 1] = feat[0]

    def rows(w):
        a = np.zeros(w.shape[:-1] + (32,), w.dtype)
        for k in range(3):
            a[..., 8 * k:8 * k + 8] = w
        return a
    wq = rows(g["attn_b_Wq"].reshape(D, HB, DB)).reshape(D, 512)
    wk = rows(np.repeat(g["attn_b_Wk"][:, None, :], 4, 1)).reshape(D, 128)
    w_b = np.concatenate([wq, wk, g["attn_b_Wo"]], 1)
    bq = rows(g["attn_b_bq"].reshape(HB, DB)).reshape(4, 128)
    bk = rows(np.repeat(g["attn_b_bk"][None], 4, 0))
    bk[:, 24:26] = 1.0
    bias_b = np.concatenate([bq, bk.reshape(1, 128), np.zeros((1, 128), np.float32)], 0).T
    low = np.zeros((128, 2), np.float32)
    for q in range(4):
        low[32 * q + 8:32 * q + 16, 0] = -1.0
        low[32 * q + 16:32 * q + 24, 1] = -1.0
    arrays = {
        "q": g["attn_a_q"].reshape(B * L, D),
        "w_qs": g["attn_a_w_qs"], "w_ks": g["attn_a_w_ks"], "w_vs": g["attn_a_w_vs"],
        "w_rel": g["attn_a_w_rel_pos_k"], "w_out": g["attn_a_w_out"], "bo_a": g["attn_a_b_out"],
        "bias_a": np.concatenate([g["attn_a_rel_embed_bias"].reshape(H, DK), g["attn_a_rel_pos_bias"].reshape(H, DK)], 0).T,
        "feat": ft, "feat0": f0,
        "w_b": w_b, "wv_b": g["attn_b_Wv"], "bias_b": bias_b,
        "bvo_b": np.concatenate([g["attn_b_bv"], g["attn_b_bo"]]), "low": low,
        "wgt": g["ffn_Wg"].T, "w1t": g["ffn_W1"].transpose(2, 0, 1).reshape(D, E * 512),
        "b1": g["ffn_b1"].reshape(-1), "wo_f": g["ffn_Wo"].T, "bo_f": g["ffn_bo"],
    }
    nc = bacc.Bacc("TRN2", target_bir_lowering=False, num_devices=1, dynamic_dma_scratch_size=1024)
    arrays = {k: np.ascontiguousarray(v) for k, v in arrays.items()}
    dram = {k: nc.dram_tensor(f"in_{k}", v.shape, mybir.dt.from_np(v.dtype), kind="ExternalInput").ap()
            for k, v in arrays.items()}
    dram["out"] = nc.dram_tensor("out_0", (B * L, D), F32, kind="ExternalOutput").ap()
    build(nc, dram)
    r = run_bass_kernel_spmd(nc, [{f"in_{k}": v for k, v in arrays.items()}], core_ids=[0])
    return np.asarray(r.results[0]["out_0"]).reshape(B, L, D)
```

```python
import math
from contextlib import ExitStack

import numpy as np
import concourse.bass as bass
from concourse import mybir
from concourse.alu_op_type import AluOpType as ALU

F32 = mybir.dt.float32
F32R = mybir.dt.float32r
BF16 = mybir.dt.bfloat16
U32 = mybir.dt.uint32
ACT = mybir.ActivationFunctionType
AX = mybir.AxisListType.X

B, L, D = 4, 1024, 128
NT = B * L // 128
H, DK = 8, 128
NF = 96
E, FH = 8, 256
HB, DB = 16, 8
EPS_LN = 1e-5
EPS_TOPK = 1e-9
RW = 1152
NSP = 9
NP = 7
AHEAD = 15
NEG = -1e30


class Token:

    def __init__(self, sem=None, value=None):
        self.sem, self.value, self.used = sem, value, sem is not None


class Queue:

    def __init__(self, sem):
        self.sem, self.items = sem, []

    def op(self, emit, *waits):
        flat = []
        for w in waits:
            flat += w if isinstance(w, (list, tuple)) else [w]
        flat = [w for w in flat if w is not None]
        for w in flat:
            w.used = True
        t = Token()
        self.items.append((flat, emit, t))
        return t

    def last(self):
        return [i[2] for i in self.items[-1:]]

    def number(self):
        n = 0
        for _, _, t in self.items:
            if t.sem is None and t.used:
                n += 1
                t.sem, t.value = self.sem, n

    def play(self, eng):
        seen = {}
        for waits, emit, t in self.items:
            need = {}
            for w in waits:
                if w.value > seen.get(w.sem.name, (None, 0))[1]:
                    if w.value > need.get(w.sem.name, (None, 0))[1]:
                        need[w.sem.name] = (w.sem, w.value)
            for name, (s, v) in need.items():
                eng.wait_ge(s, v)
                seen[name] = (s, v)
            ins = emit(eng)
            if t.sem is self.sem and t.used:
                ins.then_inc(self.sem, 1)


class DmaSem:

    def __init__(self, sem):
        self.sem, self.value = sem, 0

    def start(self, queue, out, in_, *waits):
        self.value += 16
        t = Token(self.sem, self.value)
        queue.op(lambda e: e.dma_start(out, in_).then_inc(self.sem, 16), *waits)
        return t


class Bank:

    def __init__(self, n):
        self.n, self.free = n, None


class Program:
    def __init__(self, nc, dram):
        self.nc, self.dr = nc, dram
        self.ctx = ExitStack()

    def sem(self, name):
        return self.ctx.enter_context(self.nc.semaphore(name))

    def fence(self):
        t = []
        for q in (self.pe, self.act, self.dve, self.pool):
            t += q.last()
        return t + self.dma_tokens

    def dma(self, out, in_, *waits, sem=None):
        if sem is None:
            sem = DmaSem(self.sem(f"dma{self.ndma}"))
            self.ndma += 1
        t = sem.start(self.sp, out, in_, *waits)
        return t

    def build(self):
        nc = self.nc
        with self.ctx:
            self.pe, self.act, self.dve, self.pool, self.sp = (
                Queue(self.sem("s_" + n)) for n in ("pe", "act", "dve", "pool", "sp"))
            self.ndma, self.dma_tokens = 0, []
            keep = self.ctx
            self.ps = keep.enter_context(nc.psum_tensor("ps", [128, 8, 512], F32))
            self.x = keep.enter_context(nc.sbuf_tensor("x", [128, NT, 128], F32))
            self.ident = keep.enter_context(nc.sbuf_tensor("ident", [128, 128], F32))
            self.maskq = keep.enter_context(nc.sbuf_tensor("maskq", [128, 512], F32))
            self.iota = keep.enter_context(nc.sbuf_tensor("iota", [128, E], F32))
            self.lowmask = keep.enter_context(nc.sbuf_tensor("lowmask", [128, 2], F32))
            sbp = lambda n, s, d: keep.enter_context(nc.sbuf_tensor("p_" + n, s, d))
            self.xh, self.xl = sbp("xh", [128, B * L], F32R), sbp("xl", [128, B * L], F32R)
            self.xn = sbp("xn", [128, 4, 128], F32)
            self.st, self.mv = sbp("st", [128, 8, 6], F32), sbp("mv", [128, 8, 2], F32)
            self.ve, self.sd, self.rs = (sbp(n, [128, 8], F32) for n in ("ve", "sd", "rs"))
            self.wgh, self.wgl = sbp("wgh", [128, E], F32R), sbp("wgl", [128, E], F32R)
            self.wgs, self.wgr = sbp("wgs", [128, E], F32), sbp("wgr", [128, E], F32)
            self.lg, self.ex, self.v8, self.oht = (sbp(n, [128, 8, E], F32) for n in ("lg", "ex", "v8", "oht"))
            self.i8 = sbp("i8", [128, 8, 8], U32)
            self.if8, self.pv2 = sbp("if8", [128, 8, 2], F32), sbp("pv2", [128, 8, 2], F32)
            self.sm, self.den = sbp("sm", [128, 8], F32), sbp("den", [128, 8], F32)
            self.comb = sbp("comb", [128, NT, E], F32)
            self.csum = sbp("csum", [128, NT], F32)
            self.t_xn, self.t_comb, self.t_res = [None] * B, [None] * B, [None] * B
            self.n_end, self.t_done = None, []
            self.constants()
            xin = self.dr["q"].rearrange("(n p) d -> p n d", p=128)
            self.t_x = [self.dma(self.x[:, 0:8, :], xin[:, 0:8, :])]

            self.attention_a()
            more = self.rest()
            self.ffn(False, more)
            self.attention_b()
            self.ffn(True)
            for t in self.t_done:
                self.sp.op(lambda e, t=t: e.wait_ge(t.sem, t.value))

            for q in (self.pe, self.act, self.dve, self.pool, self.sp):
                q.number()
            block = self.ctx.enter_context(nc.Block())
            block.sync(lambda e: self.sp.play(e))
            block.tensor(lambda e: self.pe.play(e))
            block.scalar(lambda e: self.act.play(e))
            block.vector(lambda e: self.dve.play(e))
            block.gpsimd(lambda e: self.pool.play(e))

    def rest_of_inputs(self):
        xin = self.dr["q"].rearrange("(n p) d -> p n d", p=128)
        self.t_x += [self.dma(self.x[:, 8 * b:8 * b + 8, :], xin[:, 8 * b:8 * b + 8, :]) for b in range(1, B)]
        self.t_low = self.dma(self.lowmask[:, :], self.dr["low"])
        t = self.dma(self.wgs[:, :], self.dr["wgt"])
        t = self.dve.op(lambda e: e.tensor_tensor(self.wgs[:, :], self.wgs[:, :], self.wgr[:, :], ALU.subtract),
                        t, self.last_row(self.wgr, "wgr"))
        self.t_wg = self.split(self.wgh[:, :], self.wgl[:, :], self.wgs[:, :], t)

    def constants(self):
        p = self.pool
        cond = dict(pattern=[[-1, 128]], channel_multiplier=1, base=0)
        a = p.op(lambda e: e.memset(self.ident[:, :], 0.0))
        c = p.op(lambda e: e.memset(self.maskq[:, :], 0.0))
        self.t_ident = p.op(lambda e: e.affine_select(out=self.ident[:, :], in_=self.ident[:, :],
                            compare_op=ALU.not_equal, fill=1.0, **cond), a)
        self.t_mask = p.op(lambda e: e.affine_select(out=self.maskq[:, 384:512], in_=self.maskq[:, 384:512],
                           compare_op=ALU.is_ge, fill=NEG, **cond), c)
        self.t_const = p.op(lambda e: e.iota(self.iota[:, :], pattern=[[1, E]], base=0, channel_multiplier=0,
                                             allow_small_or_imprecise_dtypes=True))

    def last_row(self, out, name, *waits, cs=slice(0, E)):
        v = self.dr[name][:, cs]
        return [self.dma(out[0:127, :], bass.AP(v.tensor, v.offset, [[0, 127], [1, cs.stop - cs.start]]), *waits),
                self.dma(out[127:128, :], v[1:2, :], *waits)]

    def split(self, hi, lo, src, *waits, eng=None):
        a = self.act.op(lambda e: e.activation(hi, src, ACT.Copy), *waits)
        b = self.dve.op(lambda e: e.tensor_tensor(lo, src, hi.bitcast(F32), ALU.subtract), a)
        return [a, b]

    def mm3(self, e, out, lh, ll, rh, rl):
        e.matmul(out, lh, rh, start=True, stop=False)
        e.matmul(out, lh, rl, start=False, stop=False)
        return e.matmul(out, ll, rh, start=False, stop=True)

    def norm(self, b, X, ready, one=False):
        x, DV = self.x, self.dve
        h = {}

        def stats():
            for n in range(8):
                t = DV.op(lambda e, n=n: e.bn_stats(self.st[:, n, :], x[:, 8 * b + n, :]), ready() if n == 0 else None)
            h["b"] = t

        def total():
            for n in range(8):
                t = DV.op(lambda e, n=n: e.bn_aggr(self.mv[:, n, :], self.st[:, n, :]), h["b"])
            t = DV.op(lambda e: e.tensor_scalar(self.ve[:, :], self.mv[:, :, 1], EPS_LN, None, ALU.add), t)
            h["s"] = self.act.op(lambda e: e.activation(self.sd[:, :], self.ve[:, :], ACT.Sqrt), t)

        def scale(half):
            if half == 0:
                h["r"] = DV.op(lambda e: e.reciprocal(self.rs[:, :], self.sd[:, :]), h["s"])
            for k in range(4):
                n = 4 * half + k
                h["x"] = DV.op(lambda e, k=k, n=n: e.tensor_scalar(self.xn[:, k, :], x[:, 8 * b + n, :], self.mv[:, n, 0:1],
                               self.rs[:, n:n + 1], ALU.subtract, ALU.mult), h["r"], self.n_end)
            if one:
                h["x"] = DV.op(lambda e: e.memset(self.xn[:, :, 127:128], 1.0), h["x"])

        def turn(half):
            def emit(e):
                for k in range(4):
                    i = e.transpose(self.ps[:, X.n, 128 * k:128 * k + 128], self.xn[:, k, :], self.ident[:, :])
                return i
            self.n_end = self.pe.op(emit, h["x"], X.free, self.t_ident)
            cs = slice(L * b + 512 * half, L * b + 512 * half + 512)
            r = self.split(self.xh[:, cs], self.xl[:, cs], self.ps[:, X.n, :], self.n_end)
            X.free = r[1]
            if half == 0:
                self.t_xn[b] = [None, None]
            self.t_xn[b][half] = r
        return [(stats, ()), (total, ()), (scale, (0,)), (turn, (0,)), (scale, (1,)), (turn, (1,))]

    def gate(self, b, X):
        DV = self.dve
        h = {}
        lb = self.ps[:, X.n, 0:8 * E].rearrange("p (n e) -> p n e", e=E)

        def bc(v, n):
            y = v[:, :]
            return bass.AP(y.tensor, y.offset, [y.ap[0], [1, 8], [0, n]])

        def logits():
            def emit(e):
                for n in range(8):
                    cs = slice(L * b + 128 * n, L * b + 128 * n + 128)
                    i = self.mm3(e, lb[:, n, :], self.xh[:, cs], self.xl[:, cs], self.wgh[:, :], self.wgl[:, :])
                return i
            p = self.pe.op(emit, self.t_wg, *self.t_xn[b], X.free)
            h["l"] = X.free = DV.op(lambda e: e.tensor_copy(self.lg[:, :, :], lb), p)

        def best():
            for n in range(8):
                t = DV.op(lambda e, n=n: e.max(self.v8[:, n, :], self.lg[:, n, :]), h["l"])
            h["m"] = t

        def place():
            for n in range(8):
                t = DV.op(lambda e, n=n: e.max_index(self.i8[:, n, :], self.v8[:, n, :], self.lg[:, n, :]), h["m"])
            v = self.v8[:, 0, :]
            top = bass.AP(v.tensor, v.offset, [v.ap[0], [8, 8], [0, E]])
            top2 = bass.AP(v.tensor, v.offset, [v.ap[0], [8, 8], [0, 2]])
            a = DV.op(lambda e: e.tensor_tensor(self.ex[:, :, :], self.lg[:, :, :], top, ALU.subtract), t)
            c = DV.op(lambda e: e.tensor_tensor(self.pv2[:, :, :], self.v8[:, :, 0:2], top2, ALU.subtract))
            h["u"] = DV.op(lambda e: e.tensor_copy(self.if8[:, :, :], self.i8[:, :, 0:2]))
            self.act.op(lambda e: e.activation(self.ex[:, :, :], self.ex[:, :, :], ACT.Exp), a)
            h["e"] = self.act.op(lambda e: e.activation(self.pv2[:, :, :], self.pv2[:, :, :], ACT.Exp), c)

        def share():
            pv, sm, den = self.pv2, self.sm, self.den
            t = DV.op(lambda e: e.reduce_sum(sm[:, :], self.ex[:, :, :], axis=AX), h["e"])
            t = DV.op(lambda e: e.reciprocal(sm[:, :], sm[:, :]), t)
            t = DV.op(lambda e: e.tensor_tensor(pv[:, :, :], pv[:, :, :], bc(sm, 2), ALU.mult), t)
            t = DV.op(lambda e: e.tensor_tensor(den[:, :], pv[:, :, 0], pv[:, :, 1], ALU.add), t)
            t = DV.op(lambda e: e.tensor_scalar(den[:, :], den[:, :], EPS_TOPK, None, ALU.add), t)
            t = DV.op(lambda e: e.reciprocal(den[:, :], den[:, :]), t)
            h["t"] = DV.op(lambda e: e.tensor_tensor(pv[:, :, :], pv[:, :, :], bc(den, 2), ALU.mult), t)

        def combine():
            io = self.iota[:, :]
            iob = bass.AP(io.tensor, io.offset, [io.ap[0], [0, 8], [1, E]])
            cb = self.comb[:, 8 * b:8 * b + 8, :]
            for k, dst in ((0, cb), (1, self.oht[:, :, :])):
                ik, vk = self.if8[:, :, k], self.pv2[:, :, k]
                ib = bass.AP(ik.tensor, ik.offset, [ik.ap[0], [2, 8], [0, E]])
                vb = bass.AP(vk.tensor, vk.offset, [vk.ap[0], [2, 8], [0, E]])
                w = DV.op(lambda e, ib=ib, dst=dst: e.tensor_tensor(dst, iob, ib, ALU.is_equal), h["u"], self.t_const)
                t = DV.op(lambda e, vb=vb, dst=dst: e.tensor_tensor(dst, dst, vb, ALU.mult), w, h["t"])
            t = DV.op(lambda e: e.tensor_tensor(cb, cb, self.oht[:, :, :], ALU.add), t)
            self.t_comb[b] = DV.op(lambda e: e.reduce_sum(self.csum[:, 8 * b:8 * b + 8], cb, axis=AX), t)
        return [(logits, ()), (best, ()), (place, ()), (share, ()), (combine, ())]

    def attention_a(self):
        nc, ps, x, dr = self.nc, self.ps, self.x, self.dr
        PE, AC, DV = self.pe, self.act, self.dve
        c = ExitStack()
        with c:
            sb = lambda n, s, d: c.enter_context(nc.sbuf_tensor("a_" + n, s, d))
            xh, xl = self.xh, self.xl
            fh, fl = sb("fh", [NF, 2048], F32R), sb("fl", [NF, 2048], F32R)
            zh, zl = sb("zh", [NF, 2], F32R), sb("zl", [NF, 2], F32R)
            rh, rl = sb("rh", [128, 2048], F32R), sb("rl", [128, 2048], F32R)
            Kh, Kl = sb("Kh", [128, 2, L], F32R), sb("Kl", [128, 2, L], F32R)
            Vh, Vl = sb("Vh", [128, 2, L], F32R), sb("Vl", [128, 2, L], F32R)
            Qh, Ql = sb("Qh", [128, 2, 2, 512], F32R), sb("Ql", [128, 2, 2, 512], F32R)
            Ph, Pl = sb("Ph", [128, 3, 512], F32R), sb("Pl", [128, 3, 512], F32R)
            osb = sb("osb", [128, 512], F32)
            vth, vtl = sb("vth", [128, 128], F32R), sb("vtl", [128, 128], F32R)
            rt = sb("rt", [128, 2, RW], F32)
            sp = sb("sp", [128, NSP, L], F32)
            wst = sb("wst", [128, 4, 128], F32)
            wh, wl = sb("wh", [128, 2, 4, 128], F32R), sb("wl", [128, 2, 4, 128], F32R)
            gst = sb("gst", [NF, 2, 128], F32)
            gsm = sb("gsm", [NF, 3, 128], F32)
            gh, gl = sb("gh", [NF, 2, 3, 128], F32R), sb("gl", [NF, 2, 3, 128], F32R)
            bias = sb("bias", [128, 2, H], F32)
            nm = sb("nm", [128, 8], F32)
            ls = sb("ls", [128, 16], F32)
            rv = sb("rv", [128, 8], F32)
            bo = sb("bo", [128, 128], F32)
            scr = nc.dram_tensor("scr", (4, 128, RW), F32, kind="Internal").ap()

            X = Bank(7)
            more = [Bank(n) for n in range(2, 7)]
            t_xb = {}

            def bout(b):
                y = bo[:, :]
                t_xb[b] = DV.op(lambda e: e.tensor_tensor(x[:, 8 * b:8 * b + 8, :], x[:, 8 * b:8 * b + 8, :],
                                bass.AP(y.tensor, y.offset, [y.ap[0], [0, 8], [1, 128]]), ALU.add), t_bo)
            t_fs = []

            def split_features():
                t_fs.extend(self.split(fh[:, :], fl[:, :], fst, t_f) + self.split(zh[:, :], zl[:, :], zst, t_z))

            s_w, s_g = DmaSem(self.sem("s_w")), DmaSem(self.sem("s_g"))
            s_wr = [DmaSem(self.sem(f"s_wr{i}")) for i in range(4)]
            s_rd = [DmaSem(self.sem(f"s_rd{i}")) for i in range(NSP)]

            SC = float(DK) ** -0.5
            NTI = H * NT
            t_wt, t_wv, t_vt, t_out = {}, {}, [None], {}
            st_free, t_ld = [[]], {}

            def load(h):
                hs, free = slice(128 * h, 128 * h + 128), st_free[0]
                for k, nme in enumerate(("w_qs", "w_ks", "w_vs")):
                    tw = s_w.start(self.sp, wst[:, k, :], dr[nme][:, hs], *free)
                tw = s_w.start(self.sp, wst[:, 3, :], dr["w_out"][hs, :], *free)
                tg = s_g.start(self.sp, gst[:, :, :], dr["w_rel"][:, hs].rearrange("(a p) n -> p a n", p=NF), *free)
                t_ld[h] = tw, tg

            def weights(h):
                s, (tw, tg) = h % 2, t_ld[h]
                free = st_free[0] + [t_out.get(4 * 2 * h - 9)]
                a = DV.op(lambda e: e.tensor_scalar(wst[:, 0, :], wst[:, 0, :], SC, None, ALU.mult), tw)
                b = [DV.op(lambda e: e.tensor_tensor(gsm[:, 0, :], gst[:, 0, :], gst[:, 1, :], ALU.subtract), tg, free),
                     DV.op(lambda e: e.tensor_tensor(gsm[:, 1, :], gst[:, 0, :], gst[:, 1, :], ALU.add)),
                     DV.op(lambda e: e.tensor_copy(gsm[:, 2, :], gst[:, 1, :]))]
                r = self.split(wh[:, s, :, :], wl[:, s, :, :], wst[:, :, :], a, free)
                r += self.split(gh[:, s, :, :], gl[:, s, :, :], gsm[:, :, :], b, free)
                st_free[0] = r
                t_wt[h] = r
                t_wv[h] = tw

            def valueweights(h, part, X=X):
                s, out = h % 2, ps[:, X.n, 0:128]
                if part == 0:
                    p = PE.op(lambda e: e.transpose(out, wst[:, 2, :], self.ident[:, :]), t_wv[h], X.free, self.t_ident)
                    st_free[0] = st_free[0] + [p]
                    t_vt[0] = self.split(vth[:, :], vtl[:, :], out, p)
                    X.free = t_vt[0][1]
                else:
                    p = PE.op(lambda e: self.mm3(e, out, vth[:, :], vtl[:, :], wh[:, s, 3, :], wl[:, s, 3, :]),
                              t_vt[0], t_wt[h], X.free)
                    t_wv[h] = self.split(wh[:, s, 2, :], wl[:, s, 2, :], out, p)
                    X.free = t_wv[h][1]

            load(0)
            weights(0)
            fst = sp[0:NF, 0:2, :].rearrange("p a n -> p (a n)")
            t_f = self.dma(fst, dr["feat"])
            zst = sp[0:NF, 2, 0:2]
            t_z = self.dma(zst, dr["feat0"])
            self.rest_of_inputs()
            t_bo = self.dma(bo[:, :], bass.AP(dr["bo_a"].tensor, 0, [[0, 128], [1, 128]]))
            t_bias = self.dma(bias[:, :, :], dr["bias_a"].rearrange("d (a h) -> d a h", a=2))
            OB = ps[:, 6, :]
            rbank_free, tb_free, s_free, o_free = [None, None], [None, None], [None], [None]
            t_rel, t_q, t_k, t_v = [None] * 8, {}, {}, {}
            pe_R, pe_S, pe_T, pe_PV, pe_OUT = {}, {}, {}, {}, {}
            t_rd, t_wd, t_add, t_exp, t_PT, t_lo = {}, {}, {}, {}, {}, {}
            rev = {}

            def relunit(h, u, X=X):
                s, cs = h % 2, slice(256 * u, 256 * u + 256)
                g = 0 if u < 4 else 1
                out = ps[:, X.n, 0:256]

                def emit(e):
                    i = self.mm3(e, out, gh[:, s, g, :], gl[:, s, g, :], fh[:, cs], fl[:, cs])
                    if u == 3:
                        i = self.mm3(e, ps[:, X.n, 256:258], gh[:, s, 2, :], gl[:, s, 2, :], zh[:, :], zl[:, :])
                    return i
                p = PE.op(emit, X.free, t_wt[h], t_fs)
                last = pe_R.get(max(pe_R)) if pe_R else None
                if u == 3:
                    fix = DV.op(lambda e: e.tensor_copy(rv[:, 6:7], ps[:, X.n, 257:258]), p)
                    p = DV.op(lambda e: e.tensor_tensor(ps[:, X.n, 255:256], ps[:, X.n, 255:256], rv[:, 6:7], ALU.add), fix)
                t_rel[u] = self.split(rh[:, cs], rl[:, cs], out, p, last)
                X.free = t_rel[u][1]

            def qunit(qd, X=X):
                XB = ps[:, X.n, :]
                h, s = qd // 8, qd % 2
                cols = slice(512 * (qd % 8), 512 * (qd % 8) + 512)
                p = PE.op(lambda e: self.mm3(e, XB, wh[:, h % 2, 0, :], wl[:, h % 2, 0, :], xh[:, cols], xl[:, cols]),
                          X.free, t_wt[h], self.t_xn[(qd % 8) // 2][qd % 2])
                war = [pe_S.get(4 * qd - 5), pe_R.get(4 * qd - 5)]
                a = [AC.op(lambda e, k=k: e.activation(Qh[:, s, k, :], XB, ACT.Identity, bias=bias[:, k, h:h + 1]),
                           p, war, t_bias) for k in range(2)]
                d = [DV.op(lambda e, k=k: e.scalar_tensor_tensor(Ql[:, s, k, :], XB, bias[:, k, h:h + 1],
                           Qh[:, s, k, :].bitcast(F32), ALU.add, ALU.subtract), a) for k in range(2)]
                t_q[qd] = a + d
                X.free = d[1]

            def kunit(bh, half, X=X):
                XB = ps[:, X.n, :]
                h, b, s = bh // B, bh % B, bh % 2
                cols = slice(L * b + 512 * half, L * b + 512 * half + 512)
                p = PE.op(lambda e: self.mm3(e, XB, wh[:, h % 2, 1, :], wl[:, h % 2, 1, :], xh[:, cols], xl[:, cols]),
                          X.free, t_wt[h], self.t_xn[b][half])
                o = slice(512 * half, 512 * half + 512)
                r = self.split(Kh[:, s, o], Kl[:, s, o], XB, p, pe_S.get(8 * (bh - 1) - 1))
                t_k.setdefault(bh, []).extend(r)
                X.free = r[1]

            def vunit(bh, half, X=X):
                XB = ps[:, X.n, :]
                h, b, s = bh // B, bh % B, bh % 2

                def emit(e):
                    for j in range(4):
                        cs = slice(L * b + 512 * half + 128 * j, L * b + 512 * half + 128 * j + 128)
                        i = self.mm3(e, XB[:, 128 * j:128 * j + 128], xh[:, cs], xl[:, cs],
                                     wh[:, h % 2, 2, :], wl[:, h % 2, 2, :])
                    return i
                p = PE.op(emit, X.free, t_wv[h], self.t_xn[b][half])
                o = slice(512 * half, 512 * half + 512)
                r = self.split(Vh[:, s, o], Vl[:, s, o], XB, p, pe_PV.get((2 * (bh - 1) - 1, 7)))
                t_v[bh, half] = r
                X.free = r[1]

            def rchunk(t, k):
                I, qd, s = t % 8, t // 4, (t // 4) % 2
                qs = slice(128 * (t % 4), 128 * (t % 4) + 128)
                rb = (3 * t + k) % 2
                cs = slice(896 - 128 * I + 384 * k, 896 - 128 * I + 384 * k + 384)
                units = [t_rel[u] for u in range(cs.start // 256, (cs.stop - 1) // 256 + 1)]
                pe_R[t] = PE.op(lambda e: self.mm3(e, ps[:, rb, 0:384], Qh[:, s, 1, qs], Ql[:, s, 1, qs],
                                rh[:, cs], rl[:, cs]), rbank_free[rb], t_q[qd], *units)
                rev.setdefault(t, []).append((pe_R[t], rt[:, t % 2, 384 * k:384 * k + 384], ps[:, rb, 0:384],
                                              [t_wd.get(t - 2)], rb))

            def revac(t, k):
                p, dst, src, war, rb = rev[t][k]
                if k == 1:
                    a = DV.op(lambda e: e.tensor_copy(dst, src), p, war)
                else:
                    a = AC.op(lambda e: e.activation(dst, src, ACT.Copy), p, war)
                rbank_free[rb] = a
                rev[t][k] = a

            def rwrite(t):
                t_wd[t] = s_wr[t % 4].start(self.sp, scr[t % 4, :, :], rt[:, t % 2, :], rev[t], t_rd.get(t - 4))

            def rread(t):
                src = bass.AP(scr.tensor, (t % 4) * 128 * RW + 127, [[RW - 1, 128], [1, L]])
                t_rd[t] = s_rd[t % NSP].start(self.sp, sp[:, t % NSP, :], src, t_wd[t], pe_T.get(((t - NSP) // 4, 7)), t_fs)

            def stile(t):
                bh, qd = t // 8, t // 4
                s, q2 = bh % 2, qd % 2
                qs = slice(128 * (t % 4), 128 * (t % 4) + 128)

                def emit(e):
                    for k in range(2):
                        cs = slice(512 * k, 512 * k + 512)
                        i = self.mm3(e, ps[:, 2 + k, :], Qh[:, q2, 0, qs], Ql[:, q2, 0, qs], Kh[:, s, cs], Kl[:, s, cs])
                    return i
                pe_S[t] = PE.op(emit, s_free[0], t_q[qd], t_k[bh])
                w = sp[:, t % NSP, :]
                t_add[t] = DV.op(lambda e: e.tensor_tensor_reduce(
                    out=w, in0=ps[:, 2:4, :].rearrange("p a n -> p (a n)"), in1=w, scale=-1.0, scalar=3e38,
                    op0=ALU.add, op1=ALU.min, accum_out=nm[:, t % 8:t % 8 + 1]), pe_S[t], t_rd[t], t_exp.get(t - 8))
                s_free[0] = t_add[t]

            def softmax(t):
                w = sp[:, t % NSP, :]
                t_exp[t] = AC.op(lambda e: e.activation(w, w, ACT.Exp, bias=nm[:, t % 8:t % 8 + 1], scale=-1.0,
                                 accum_out=ls[:, t % 16:t % 16 + 1]), t_add[t], t_out.get(t // 4 - 4))

            def tblock(qd, j):
                bank, slot = 4 + j % 2, (8 * qd + j) % 3

                def emit(e):
                    for k in range(4):
                        i = e.transpose(ps[:, bank, 128 * k:128 * k + 128],
                                        sp[:, (4 * qd + k) % NSP, 128 * j:128 * j + 128], self.ident[:, :])
                    return i
                p = PE.op(emit, *[t_exp[4 * qd + k] for k in range(4)], tb_free[j % 2])
                pe_T[qd, j] = p
                a = AC.op(lambda e: e.activation(Ph[:, slot, :], ps[:, bank, :], ACT.Copy), p,
                          pe_PV.get((qd, j - 3) if j > 2 else (qd - 1, j + 5)))
                t_PT[qd, j] = a

            def tlow(qd, j):
                bank, slot = 4 + j % 2, (8 * qd + j) % 3
                a = t_PT[qd, j]
                d = DV.op(lambda e: e.tensor_tensor(Pl[:, slot, :], ps[:, bank, :], Ph[:, slot, :].bitcast(F32),
                          ALU.subtract), a)
                tb_free[j % 2] = d
                t_PT[qd, j] = [a, d]

            def pv(qd, j):
                bh = qd // 2
                s, slot = bh % 2, (8 * qd + j) % 3
                cs = slice(128 * j, 128 * j + 128)

                def emit(e):
                    e.matmul(OB, Vh[:, s, cs], Ph[:, slot, :], start=j == 0, stop=False)
                    e.matmul(OB, Vh[:, s, cs], Pl[:, slot, :], start=False, stop=False)
                    return e.matmul(OB, Vl[:, s, cs], Ph[:, slot, :], start=False, stop=j == 7)
                pe_PV[qd, j] = PE.op(emit, t_PT[qd, j], t_v[bh, j // 4], o_free[0] if j == 0 else None)
                if j == 7:
                    o_free[0] = t_lo[qd] = AC.op(lambda e: e.activation(osb[:, :], OB, ACT.Copy), pe_PV[qd, 7], pe_OUT.get(qd - 1))

            def output(qd):
                def emit(e):
                    for k in range(4):
                        i = e.transpose(ps[:, 7, 128 * k:128 * k + 128], osb[:, 128 * k:128 * k + 128], self.ident[:, :])
                    return i
                pe_OUT[qd] = PE.op(emit, t_lo[qd], X.free)
                c4 = (4 * qd) % 16
                r = DV.op(lambda e: e.reciprocal(rv[:, 0:4], ls[:, c4:c4 + 4]), t_exp[4 * qd + 3], t_out.get(qd - 1))
                for k in range(4):
                    n = 4 * (qd % 8) + k
                    t = DV.op(lambda e, k=k, n=n: e.scalar_tensor_tensor(
                        x[:, n, :], ps[:, 7, 128 * k:128 * k + 128], rv[:, k:k + 1], x[:, n, :], ALU.mult, ALU.add),
                        r, pe_OUT[qd], t_xb[(qd % 8) // 2])
                t_out[qd] = t
                X.free = t

            for f, a in self.norm(0, more[4], lambda: self.t_x[0]):
                f(*a)
            bout(0)
            split_features()
            valueweights(0, 0)
            qunit(0, more[0])
            kunit(0, 0, more[1])
            valueweights(0, 1)
            kunit(0, 1, more[2])
            for i, u in enumerate((7, 6, 5, 4)):
                relunit(0, u, more[(3 + i) % 5])
            for half in range(2):
                vunit(0, half, more[(2 + half) % 5])
            for i, u in enumerate((3, 2, 1, 0)):
                relunit(0, u, more[(4 + i) % 5])
            s_free[0] = [more[0].free, more[1].free]
            tb_free[:] = [more[2].free, more[3].free]
            o_free[0] = more[4].free
            for t in range(3):
                for k in range(3):
                    rchunk(t, k)
                    revac(t, k)
                rwrite(t)
                if t:
                    rread(t - 1)
            REL = {-1: (7,), 1: (6,), 3: (5,), 4: (4, 3), 6: (2,), 8: (1,), 10: (0,)}
            rel_at = {}
            for h in range(1, H):
                for ds, us in REL.items():
                    rel_at.setdefault(8 * (4 * h - 1) + ds, []).extend((h, u) for u in us)
            NQ = NTI // 4
            extra = {}
            for b in range(1, B):
                todo = self.norm(b, X, lambda b=b: self.t_x[b]) + [(bout, (b,))]
                for i, it in enumerate(todo):
                    extra.setdefault(i // 4 if b == 1 else 8 * b - 14 + i, []).append(it)
            for b in range(B - 1):
                todo = self.norm(b, X, lambda b=b: t_out[8 * (H - 1) + 2 * b + 1], True) + self.gate(b, X)
                for i, it in enumerate(todo):
                    extra.setdefault(4 * (8 * (H - 1) + 2 * b + 3) + 1 + 3 * i // 4, []).append(it)
            for s in range(NTI + 6):
                kq, qd, bh, p = s % 4, s // 4, s // 8, s // 4 - 1
                live, ahead, tlive = s < NTI, s + 3 < NTI, 0 <= p < NQ
                ja, jb = 2 * kq, 2 * kq + 1
                if live and s % 32 == 2 and s // 32 + 1 < H:
                    load(s // 32 + 1)
                if live and s % 32 == 8 and s // 32 + 1 < H:
                    weights(s // 32 + 1)
                if live and s % 32 in (10, 12) and s // 32 + 1 < H:
                    valueweights(s // 32 + 1, s % 32 // 2 - 5)
                if live:
                    stile(s)
                if tlive:
                    tblock(p, ja)
                if kq == 0 and 0 < p <= NQ:
                    pv(p - 1, 7)
                if ahead:
                    rchunk(s + 3, 0)
                    revac(s + 3, 0)
                if live:
                    softmax(s)
                if tlive:
                    tlow(p, ja)
                if ahead:
                    rchunk(s + 3, 1)
                    revac(s + 3, 1)
                if kq and tlive:
                    pv(p, ja - 1)
                if kq == 0 and qd + 1 < NQ:
                    qunit(qd + 1)
                if kq == 1 and 0 < p <= NQ:
                    output(p - 1)
                if kq == 2 and live and bh + 1 < NTI // 8:
                    kunit(bh + 1, qd % 2)
                if kq == 3 and live:
                    if qd % 2 and bh + 1 < NTI // 8:
                        vunit(bh + 1, 0)
                    if qd % 2 == 0 and bh:
                        vunit(bh, 1)
                if tlive:
                    tblock(p, jb)
                if ahead:
                    rchunk(s + 3, 2)
                    revac(s + 3, 2)
                    rwrite(s + 3)
                if s + 2 < NTI:
                    rread(s + 2)
                if tlive:
                    tlow(p, jb)
                    pv(p, ja)
                for h, u in rel_at.get(s, ()):
                    relunit(h, u)
                for f, a in extra.get(s, ()):
                    f(*a)
            self.t_res = [t_out[8 * (H - 1) + 2 * b + 1] for b in range(B)]
            self.dma_tokens = list(t_wd.values())[-4:] + list(t_rd.values())[-4:]

    def rest(self):
        sb = lambda n, s, d: self.ctx.enter_context(self.nc.sbuf_tensor("r_" + n, s, d))
        dr, AC, DV = self.dr, self.act, self.dve
        f0 = self.fence()
        self.bank_free, self.y_free = [f0] * 8, f0
        Wh, Wl = sb("Wh", [128, E, 512], F32R), sb("Wl", [128, E, 512], F32R)
        oh, ol = sb("oh", [128, 2, 128], F32R), sb("ol", [128, 2, 128], F32R)
        bo = sb("bo", [128, 128], F32)
        y, yk = sb("y", [128, 2, 512], F32), sb("yk", [128, 2, 512], F32)
        sig = y[:, :, :].rearrange("p a (c n) -> p (a c) n", c=2)
        gt = yk[:, :, :].rearrange("p a (c n) -> p (a c) n", c=2)
        acc, acc2 = sb("acc", [128, 2, FH], F32), sb("acc2", [128, 2, FH], F32)
        ost = acc[:, 0, :].rearrange("p (k d) -> p k d", k=2)
        th, tl = sb("th", [128, 2, FH], F32R), sb("tl", [128, 2, FH], F32R)
        wh, wl = sb("wh", [128, 6, 128], F32R), sb("wl", [128, 6, 128], F32R)
        wvst = sb("wvst", [128, DB], F32)
        vh, vl = sb("vh", [128, DB], F32R), sb("vl", [128, DB], F32R)
        bq = sb("bq", [128, 6], F32)
        bvo = sb("bvo", [128, 136], F32)
        yh = sb("yh", [128, 2, 512], F32R)
        K = sb("K", [128, 2, 4, L], F32R)
        V = sb("V", [128, 2, 8, 32], F32)
        mx = sb("mx", [128, 2, 8, 4, 2], F32)
        m4, m4h = sb("m4", [128, 8, 4], F32), sb("m4h", [128, 8, 4], F32R)
        NM = sb("NM", [128, 8, 4, 32], F32)
        P = sb("P", [128, NP, 512], F32)
        os_ = sb("os", [128, 2, 512], F32)
        rl = sb("rl", [128, 2, 4, 4], F32)
        ao = sb("ao", [128, 2, 8, 128], F32)
        ah, al = sb("ah", [128, 2, 512], F32R), sb("al", [128, 2, 512], F32R)
        with ExitStack() as c:
            wst, wr = (c.enter_context(self.nc.sbuf_tensor(n, [128, E, 512], F32)) for n in ("wst", "wr"))
        Q = sb("Q", [128, 2, 4, L], F32R)
        self.f_mem = Wh, Wl, oh, ol, bo, sig, gt, acc, acc2, th, tl
        self.b_mem = wh, wl, vh, vl, bq, bvo, Q, y, yh, yk, K, V, mx, m4, m4h, NM, P, os_, rl, ao, ah, al

        w1 = dr["w1t"].rearrange("d (e h) -> d e h", e=E)
        tw = [[self.dma(wst[:, k, :], w1[:, k, :], f0)] +
              self.last_row(wr[:, k, :], "w1r", f0, cs=slice(512 * k, 512 * k + 512)) for k in range(E)]
        to = self.dma(ost, dr["wo_f"].rearrange("(k p) d -> p k d", p=128), f0)
        tb = self.dma(bo[:, :], bass.AP(dr["bo_f"].tensor, 0, [[0, 128], [1, 128]]), f0)
        t_w = []
        for k in range(E):
            d = (self.pool, DV)[k % 2].op(lambda e, k=k: e.tensor_tensor(wst[:, k, :], wst[:, k, :], wr[:, k, :], ALU.subtract), tw[k])
            t_w.append(self.split(Wh[:, k, :], Wl[:, k, :], wst[:, k, :], d, f0))
        t_o = self.split(oh[:, :, :], ol[:, :, :], ost, to, f0)
        self.t_fw = t_w, t_o, tb

        pst = P[:, 0:2, :].rearrange("p a n -> p (a n)")[:, 0:768].rearrange("p (k n) -> p k n", k=6)
        tq = self.dma(pst, dr["w_b"].rearrange("d (k n) -> d k n", k=6), f0)
        tv = self.dma(wvst[:, :], dr["wv_b"], f0)
        tbq = self.dma(bq[:, :], dr["bias_b"], f0)
        tbv = self.dma(bvo[:, :], bass.AP(dr["bvo_b"].tensor, 0, [[0, 128], [1, 136]]), f0)
        t_k0 = self.pool.op(lambda e: e.memset(K[:, :, :, :].bitcast(F32), 0.0), f0)

        def prepare():
            pre = self.split(wh[:, :, :], wl[:, :, :], pst, tq) + self.split(vh[:, :], vl[:, :], wvst[:, :], tv)
            pre.append(DV.op(lambda e: e.tensor_scalar(bq[:, 0:4], bq[:, 0:4], DB ** -0.5, None, ALU.mult), tbq))
            t_nm0 = DV.op(lambda e: e.memset(NM[:, :, :, :], 0.0), f0)
            pre.append(DV.op(lambda e: e.memset(V[:, :, :, :], 1.0), f0))
            t_m0 = DV.op(lambda e: e.memset(mx[:, :, :, :, :], NEG * 10), f0)
            self.t_bw = pre + t_w[E - 1] + [tbv], tbv, t_k0, t_nm0, t_m0
        return [(prepare, ())]

    def ffn(self, last, more=()):
        nc, ps, x, dr = self.nc, self.ps, self.x, self.dr
        PE, AC, DV = self.pe, self.act, self.dve
        PO = self.pool
        xh, xl, comb, csum = self.xh, self.xl, self.comb, self.csum
        Wh, Wl, oh, ol, bo, sig, gt, acc, acc2, th, tl = self.f_mem
        t_w, t_o, tb = self.t_fw

        hb_free, tr_free, acc2_t, merged = self.bank_free[0:4], self.bank_free[4:6], {}, {}
        acc_t = {-2: t_o}
        sig_free, gt_t, th_free = [self.y_free] * 4, [self.y_free] * 4, [None, None]
        Y, X = Bank(6), Bank(7)
        Y.free, X.free = self.bank_free[6:8]

        def merge(n):
            s = n % 2
            merged[n] = acc_t[n] = DV.op(lambda e: e.tensor_tensor(acc[:, s, :], acc[:, s, :], acc2[:, s, :], ALU.add),
                                         acc_t[n], acc2_t[n])

        def finish(n):
            s = n % 2
            bank = 4 + s

            def tr(e):
                for k in range(2):
                    i = e.transpose(ps[:, bank, 128 * k:128 * k + 128], acc[:, s, 128 * k:128 * k + 128], self.ident[:, :])
                return i
            p = PE.op(tr, acc_t[n], tr_free[s])
            r = self.split(th[:, s, :], tl[:, s, :], ps[:, bank, 0:256], p, th_free[s])
            tr_free[s] = r[1]
            acc_t[n] = p
            return s, r

        def project(n, s, r):
            yb = ps[:, 6, 0:128]

            def emit(e):
                for k in range(2):
                    cs = slice(128 * k, 128 * k + 128)
                    e.matmul(yb, th[:, s, cs], oh[:, k, :], start=k == 0, stop=False)
                    e.matmul(yb, th[:, s, cs], ol[:, k, :], start=False, stop=False)
                    i = e.matmul(yb, tl[:, s, cs], oh[:, k, :], start=False, stop=k == 1)
                return i
            p = PE.op(emit, r, t_o, Y.free)
            th_free[s] = p
            d = DV.op(lambda e: e.scalar_tensor_tensor(x[:, n, :], bo[:, :], csum[:, n:n + 1], x[:, n, :],
                      ALU.mult, ALU.add), tb, self.t_comb[n // 8], self.t_res[n // 8])
            Y.free = DV.op(lambda e: e.tensor_tensor(x[:, n, :], yb, x[:, n, :], ALU.add), d, p)
            if n % 8 == 7:
                t_end[n // 8] = Y.free
                if last:
                    xo, cs = dr["out"].rearrange("(n p) d -> p n d", p=128), slice(n - 7, n + 1)
                    self.t_done.append(self.dma(xo[:, cs, :], x[:, cs, :], Y.free))

        t_end = [None] * B
        side = self.norm(B - 1, X, lambda: self.t_res[B - 1], True) + self.gate(B - 1, X) + list(more)
        t_in = list(self.t_xn[:B - 1]) + [None]
        units = [(n, k) for n in range(NT) for k in range(E)]
        fin = {}
        for i, (n, k) in enumerate(units):
            hb = ps[:, i % 4, :]
            cs = slice(128 * n, 128 * n + 128)
            b = n // 8
            if n % 8 == 0 and k == 0:
                if b == B - 1:
                    t_in[b] = self.t_xn[b]

            def emit(e, hb=hb, cs=cs, k=k):
                e.matmul(hb, xh[:, cs], Wh[:, k, :], start=True, stop=False)
                e.matmul(hb, xh[:, cs], Wl[:, k, :], start=False, stop=False)
                return e.matmul(hb, xl[:, cs], Wh[:, k, :], start=False, stop=True)
            p = PE.op(emit, hb_free[i % 4], t_w[k], t_in[b][(n % 8) // 4])
            a = AC.op(lambda e, i=i, hb=hb: e.activation(sig[:, i % 4, :], hb[:, FH:512], ACT.Sigmoid), p, sig_free[i % 4])
            s, first = n % 2, k < 2
            dst = (acc, acc2)[k][:, s, :] if first else gt[:, i % 4, :]
            d = DV.op(lambda e, i=i, hb=hb, n=n, k=k, dst=dst: e.scalar_tensor_tensor(
                dst, hb[:, 0:FH], comb[:, n, k:k + 1], sig[:, i % 4, :], ALU.mult, ALU.mult),
                a, self.t_comb[b], (acc_t.get(n - 2), merged.get(n - 2))[k] if first else gt_t[i % 4])
            hb_free[i % 4] = sig_free[i % 4] = d
            if first:
                (acc_t, acc2_t)[k][n] = d
            elif k in (2, 4):
                acc_t[n] = gt_t[i % 4] = DV.op(lambda e, i=i, s=s: e.tensor_tensor(
                    acc[:, s, :], acc[:, s, :], gt[:, i % 4, :], ALU.add), d, acc_t[n])
            else:
                acc2_t[n] = gt_t[i % 4] = PO.op(lambda e, i=i, s=s: e.tensor_tensor(
                    acc2[:, s, :], acc2[:, s, :], gt[:, i % 4, :], ALU.add), d, acc2_t[n])
            if n and k == 1:
                merge(n - 1)
            if n and k == 3:
                fin[n - 1] = finish(n - 1)
            if n and k == 6:
                project(n - 1, *fin[n - 1])
            if i % 4 == 3 and side and n:
                f, a = side.pop(0)
                f(*a)
            if not last and n % 8 == 1 and k == 7 and n > 8:
                side += self.norm(b - 1, X, lambda b=b: t_end[b - 1])
        merge(NT - 1)
        fin[NT - 1] = finish(NT - 1)
        project(NT - 1, *fin[NT - 1])
        for f, a in side:
            f(*a)
        self.t_res = t_end
        self.bank_free = hb_free + tr_free + [Y.free, X.free]
        self.y_free = [t for t in sig_free + gt_t if isinstance(t, Token)]

    def attention_b(self):
        nc, ps, x, dr = self.nc, self.ps, self.x, self.dr
        PE, AC, DV = self.pe, self.act, self.dve
        xh, xl = self.xh, self.xl
        wh, wl, vh, vl, bq, bvo, Q, y, yh, yk, K, V, mx, m4, m4h, NM, P, os_, rl, ao, ah, al = self.b_mem
        pre, tb2, t_k0, t_nm0, t_m0 = self.t_bw
        t_xb = {}

        def bout(b):
            v = bvo[:, 8:136]
            t_xb[b] = DV.op(lambda e: e.tensor_tensor(x[:, 8 * b:8 * b + 8, :], x[:, 8 * b:8 * b + 8, :],
                            bass.AP(v.tensor, v.offset, [v.ap[0], [0, 8], [1, 128]]), ALU.add), tb2, self.t_res[b])

        XB = ps[:, 7, :]
        X = Bank(7)
        bf = self.bank_free
        X.free, st = bf[7], dict(o=bf[6])
        mfree, sfree, pfree = bf[0:3], bf[3:6], [None] * NP
        yfree, osfree, ahfree = [self.y_free, self.y_free], [None, None], [None, None]
        nmx = [0]
        nst = [0]
        nyy = [0]
        last_S, last_PV, last_AO = {}, {}, {}
        t_qk, t_q2, t_V, t_K = {}, {}, {}, {}
        hold = {"nm": None, "pv": None, ("mx", 0): None, ("mx", 1): None}

        def proj(b, g, half):
            cs = slice(L * b + 512 * half, L * b + 512 * half + 512)
            os = slice(512 * half, 512 * half + 512)
            p = PE.op(lambda e: self.mm3(e, XB, wh[:, g, :], wl[:, g, :], xh[:, cs], xl[:, cs]),
                      X.free, pre, self.t_xn[b][half])
            k = nyy[0] % 2
            nyy[0] += 1
            d = AC.op(lambda e: e.activation(y[:, k, :], XB, ACT.Identity, bias=bq[:, g:g + 1],
                      scale=DB ** -0.5 if g < 4 else 1.0), p, yfree[k])
            X.free = d
            hold["y", b, g, half] = k, AC.op(lambda e: e.activation(yh[:, k, :], y[:, k, :], ACT.Copy), d)

        def proj2(b, g, half):
            os = slice(512 * half, 512 * half + 512)
            m = 0 if g < 4 else 1
            k, a = hold["y", b, g, half]
            dst = Q[:, b % 2, g, os] if g < 4 else yk[:, half, :]
            yfree[k] = DV.op(lambda e: e.scalar_tensor_tensor(dst, yh[:, k, :].bitcast(F32), self.lowmask[:, m:m + 1],
                             y[:, k, :], ALU.mult, ALU.add), a, last_S.get(b - 2) if g < 4 else t_K.get((b - 1, half)),
                             self.t_low)
            hold["yk", half] = yfree[k]
            if g < 4:
                t_qk.setdefault((b, g), []).append(yfree[k])

        def spreadkeys(b, half, q):
            os = slice(512 * half, 512 * half + 512)
            t = AC.op(lambda e: e.activation(K[32 * q:32 * q + 32, b % 2, q, os],
                      yk[32 * q:32 * q + 32, half, :], ACT.Copy), hold["yk", half], last_S.get(b - 2), t_k0)
            t_K[b, half] = t
            t_qk.setdefault((b, 4), []).append(t)

        def values(b):
            def emit(e):
                for j in range(8):
                    cs = slice(L * b + 128 * j, L * b + 128 * j + 128)
                    i = self.mm3(e, ps[:, 7, 8 * j:8 * j + 8], xh[:, cs], xl[:, cs], vh[:, :], vl[:, :])
                return i
            p = PE.op(emit, X.free, *self.t_xn[b])
            bv = bvo[:, 0:8]
            t_V[b] = DV.op(lambda e: e.tensor_tensor(V[:, b % 2, :, 0:8], ps[:, 7, 0:64].rearrange("p (j d) -> p j d", d=8),
                           bass.AP(bv.tensor, bv.offset, [bv.ap[0], [0, 8], [1, 8]]), ALU.add), p, pre, last_PV.get(b - 2))
            X.free = t_V[b]

        def maximum(b, g, I, q, part):
            k = nmx[0] % 3
            nmx[0] += 1
            w = min(512, 128 * (I + 1) - 512 * part)
            diag = I // 4 == part

            def emit(e):
                return e.matmul(ps[:, k, 0:w], Q[:, b % 2, g, 128 * I:128 * I + 128],
                                K[:, b % 2, q, 512 * part:512 * part + w], start=True, stop=True)
            p = PE.op(emit, mfree[k], t_qk[b, g], t_qk[b, 4])
            to = mx[:, g % 2, I, q, part:part + 1]
            if diag:
                mfree[k] = DV.op(lambda e: e.tensor_tensor_reduce(
                    out=ps[:, k, 0:w], in0=ps[:, k, 0:w], in1=self.maskq[:, 512 - w:512], scale=1.0, scalar=-3e38,
                    op0=ALU.add, op1=ALU.max, accum_out=to), p, hold["mx", g % 2], t_m0, self.t_mask)
            else:
                mfree[k] = DV.op(lambda e: e.reduce_max(to, ps[:, k, 0:w], axis=AX), p, hold["mx", g % 2], t_m0)

        def shift(b, g):
            t = DV.op(lambda e: e.tensor_tensor(m4[:, :, :], mx[:, g % 2, :, :, 0], mx[:, g % 2, :, :, 1], ALU.max), *mfree)
            hold["mx", g % 2] = t
            th = DV.op(lambda e: e.tensor_scalar(m4h[:, :, :], m4[:, :, :], -1.0, None, ALU.mult), t)
            t1 = DV.op(lambda e: e.tensor_copy(NM[:, :, :, 24], m4h[:, :, :].bitcast(F32)), th, hold["nm"], t_nm0)
            t2 = DV.op(lambda e: e.scalar_tensor_tensor(NM[:, :, :, 25], m4[:, :, :], -1.0, m4h[:, :, :].bitcast(F32),
                       ALU.mult, ALU.subtract), th)
            hold["t"] = [t1, t2]

        def shift2(b, g, half):
            def tr(e):
                for k in range(4):
                    i = e.transpose(ps[:, 7, 128 * k:128 * k + 128],
                                    NM[:, 4 * half + k, :, :].rearrange("p q r -> p (q r)"), self.ident[:, :])
                return i
            hold["nm"] = PE.op(tr, hold["t"], X.free)
            os = slice(512 * half, 512 * half + 512)
            X.free = DV.op(lambda e: e.tensor_tensor(Q[:, b % 2, g, os], XB, Q[:, b % 2, g, os].bitcast(F32), ALU.add),
                            hold["nm"])
            t_q2.setdefault((b, g), []).append(X.free)

        def scores(b, g, ch, J, q):
            off = max(0, 128 * (J - 4 * ch))
            diag = J >= 4 * ch
            k = 3 + nst[0] % 3
            pt = nst[0] % NP
            nst[0] += 1

            def emit(e):
                return e.matmul(ps[:, k, off:512], K[:, b % 2, q, 128 * J:128 * J + 128],
                                Q[:, b % 2, g, 512 * ch + off:512 * ch + 512], start=True, stop=True)
            p = PE.op(emit, sfree[k - 3], t_q2[b, g][ch])
            last_S[b] = p
            sfree[k - 3] = AC.op(lambda e: e.activation(P[:, pt, off:512], ps[:, k, off:512], ACT.Exp), p, pfree[pt])
            t = sfree[k - 3]
            if diag:
                t = self.pool.op(lambda e: e.affine_select(out=P[:, pt, off:off + 128], in_=P[:, pt, off:off + 128],
                                 compare_op=ALU.is_ge, fill=0.0, pattern=[[1, 128]], channel_multiplier=-1, base=0), t)
            return pt, t

        def weighted(b, g, ch, J, pts):
            off = max(0, 128 * (J - 4 * ch))

            def emit(e):
                for q in range(4):
                    i = e.matmul(ps[32 * q:32 * q + 32, 6, off:512], V[:, b % 2, J, :], P[:, pts[q][0], off:512],
                                 start=J == 4 * ch + 3, stop=J == 0, skip_group_check=True)
                return i
            p = PE.op(emit, [t for _, t in pts], t_V[b], st["o"] if J == 4 * ch + 3 else None)
            for pt, _ in pts:
                pfree[pt] = p
            hold["pv"] = last_PV[b] = p

        def normal1(b, g, ch):
            a = AC.op(lambda e: e.activation(os_[:, ch, :], ps[:, 6, :], ACT.Copy), hold["pv"], osfree[ch])
            st["o"] = a
            hold["os", b, g, ch] = a

        def normal2(b, g, ch):
            def tr(e):
                for t in range(4):
                    i = e.transpose(ps[:, 7, 128 * t:128 * t + 128], os_[:, ch, 128 * t:128 * t + 128], self.ident[:, :])
                return i
            osfree[ch] = PE.op(tr, hold["os", b, g, ch], X.free)
            v = ps[:, 7, :].rearrange("p (t q r) -> p t q r", t=4, q=4)
            d = DV.op(lambda e: e.reciprocal(rl[:, ch, :, :], v[:, :, :, 8]), osfree[ch])
            rk = rl[:, ch, :, :]
            rb = bass.AP(rk.tensor, rk.offset, [rk.ap[0], [4, 4], [1, 4], [0, 8]])
            dst = ao[:, b % 2, 4 * ch:4 * ch + 4, 32 * g:32 * g + 32].rearrange("p t (q d) -> p t q d", q=4)
            X.free = DV.op(lambda e: e.tensor_tensor(dst, v[:, :, :, 0:8], rb, ALU.mult), d, last_AO.get(b - 2))
            hold["ao", b] = X.free

        def out1(b, half):
            def tr(e):
                for k in range(4):
                    i = e.transpose(ps[:, 7, 128 * k:128 * k + 128], ao[:, b % 2, 4 * half + k, :], self.ident[:, :])
                return i
            p = PE.op(tr, X.free, hold["ao", b])
            last_AO[b] = p
            hold["oh", half] = self.split(ah[:, half, :], al[:, half, :], XB, p, ahfree[half])
            X.free = hold["oh", half][1]

        def out2(b, half):
            def emit(e):
                for k in range(4):
                    cs = slice(128 * k, 128 * k + 128)
                    i = self.mm3(e, ps[:, 7, cs], ah[:, half, cs], al[:, half, cs], wh[:, 5, :], wl[:, 5, :])
                return i
            p = PE.op(emit, hold["oh", half], X.free)
            ahfree[half] = p
            n0 = 8 * b + 4 * half
            X.free = DV.op(lambda e: e.tensor_tensor(x[:, n0:n0 + 4, :], XB.rearrange("p (k d) -> p k d", k=4),
                            x[:, n0:n0 + 4, :], ALU.add), p, t_xb[b])
            t_end[b] = X.free

        def spread(many, few, start=0):
            r, at = list(many[:start]), 0
            rest = many[start:]
            for i, m in enumerate(rest):
                r.append(m)
                upto = len(few) * (i + 1) // len(rest)
                r += few[at:upto]
                at = upto
            return r

        def first(b):
            keys = [[(spreadkeys, (b, half, q)) for q in range(4)] for half in range(2)]
            return [(proj, (b, 4, 0)), (proj, (b, 4, 1)), (proj2, (b, 4, 0)), (proj2, (b, 4, 1))] + keys[0] + [
                (proj, (b, 0, 0)), (proj, (b, 0, 1)), (proj2, (b, 0, 0)), (proj2, (b, 0, 1))] + keys[1] + [(values, (b,))]

        def prepare(n):
            if n > 15:
                return []
            b, g = n // 4, n % 4
            m = [(maximum, (b, g, I, q, part)) for I in range(7, -1, -1) for q in range(4) for part in range(1 + I // 4)]
            p = [(o, (b, g + 1, half)) for o in (proj, proj2) for half in range(2)] if g < 3 else first(b + 1) if b + 1 < B else []
            return spread(m[:32], p) + m[32:]

        def chain(n):
            b, g = n // 4, n % 4
            m = prepare(n + 1)[:AHEAD]
            k = AHEAD // 3
            return m[:k] + [(shift, (b, g))] + m[k:2 * k] + [(shift2, (b, g, 0))] + m[2 * k:] + [(shift2, (b, g, 1))]

        def cost(f, a):
            if f is maximum:
                return 65 + min(512, 128 * (a[2] + 1) - 512 * a[4])
            return {"proj": 640, "proj2": 660, "spreadkeys": 500, "values": 2600, "shift": 500, "shift2": 800, "stats": 1600,
                    "total": 900, "scale": 1000, "turn": 600, "logits": 2600, "out2": 1300}.get(f.__name__, 600)

        def finish(n):
            b, g = n // 4, n % 4
            r, prev, pts = [], [], {}
            price, pw = [], 0

            def sc(ch, J, q):
                pts.setdefault((ch, J), []).append(scores(b, g, ch, J, q))
            for ch in range(2):
                for J in range(4 * ch + 3, -1, -1):
                    w = 512 - max(0, 128 * (J - 4 * ch))
                    r += [(sc, (ch, J, q)) for q in range(3)] + prev + [(sc, (ch, J, 3))]
                    price += [0.75 * w + 54] * 3 + [1.67 * pw] * len(prev[:1]) + [300] * len(prev[1:]) + [0.75 * w + 54]
                    pw = w
                    prev = [(lambda ch, J: weighted(b, g, ch, J, pts[ch, J]), (ch, J))]
                    if J == 0:
                        prev.append((normal1, (b, g, ch)))
            return r, prev, price

        for f, a in first(0) + prepare(0) + chain(0):
            f(*a)
        late, tail = self.norm(B - 1, X, lambda: self.t_res[B - 1]) + [(bout, (b,)) for b in range(B)], []
        t_end = [None] * B
        for n in range(16):
            b, g = n // 4, n % 4
            main, end, price = finish(n)
            main = main[:3] + tail + main[3:]
            price = price[:3] + [500] * len(tail) + price[3:]
            tail = end
            k = next(i for i, (f, a) in enumerate(main) if f is normal1 and a == (b, g, 0)) + 6
            main.insert(k, (normal2, (b, g, 0)))
            price.insert(k, 0)
            side = prepare(n + 1)[AHEAD:] + chain(n + 1) if n < 15 else []
            side = spread(side, late, 9) if side else late
            late = [(normal2, (b, g, 1))]
            if g == 3:
                late += [(o, (b, half)) for half in range(2) for o in (out1, out2)]
            if g == 0 and b:
                late += self.norm(b - 1, X, lambda b=b: t_end[b - 1], True) + self.gate(b - 1, X)
            total, ahead, done, spent = sum(price), sum(cost(f, a) for f, a in side), 0, 0
            for i, (f, a) in enumerate(main):
                f(*a)
                done += price[i]
                while i >= 4 and side and spent * total < ahead * done:
                    h, c2 = side.pop(0)
                    h(*c2)
                    spent += cost(h, c2)
            for h, c2 in side:
                h(*c2)
        for f, a in tail + late:
            f(*a)
        self.t_res = t_end
        self.bank_free = mfree + sfree + [st["o"], X.free]
        self.y_free = yfree + [t_K[B - 1, half] for half in range(2)]


def build(nc, dram):
    p = Program(nc, dram)
    p.build()


def log_gamma(x):
    f = np.float32
    co = [676.520368121885098567009190444019, -1259.13921672240287047156078755283, 771.3234287776530788486528258894,
          -176.61502916214059906584551354, 12.507343278686904814458936853, -0.13857109526572011689554707,
          9.984369578019570859563e-6, 1.50563273514931155834e-7]
    z = (x - f(1)).astype(f)
    s = np.full_like(x, f(0.99999999999980993227684700473478))
    for i, c in enumerate(co):
        s = (s + f(c) / (z + f(i + 1))).astype(f)
    t = (f(7.5) + z).astype(f)
    lt = (f(math.log(7.5)) + np.log1p((z / f(7.5)).astype(f))).astype(f)
    return (((z + f(.5) - t / lt) * lt).astype(f) + (f(math.log(math.sqrt(2 * math.pi))) + np.log(s)).astype(f)).astype(f)


def features():
    f, n = np.float32, NF // 3
    d = np.arange(0, L, dtype=f)[:, None]
    half_life = (f(2.0) ** np.linspace(3.0, math.log(L) / math.log(2.0), n).astype(f)).astype(f)
    fe = np.exp((f(-math.log(2.0)) / half_life[None, :] * d).astype(f))
    cw = (f(2.0) ** np.arange(1, n + 1, dtype=f) - f(1.0)).astype(f)
    fc = (cw[None, :] > d).astype(f)
    std = L / (2.0 * n)
    mean = np.linspace(L / n, float(L), n).astype(f)[None, :]
    conc, rate = ((mean / f(std)) ** 2).astype(f), (mean / f(std ** 2)).astype(f)
    lu = ((conc - f(1)) * np.log(np.maximum(d, f(1))) - rate * d).astype(f)
    lu[0] = -np.inf
    ln = (log_gamma(conc) - (conc * np.log(rate)).astype(f)).astype(f)
    pr = (np.exp((lu - ln).astype(f)) + f(1e-8)).astype(f)
    return np.concatenate([fe, fc, pr / pr.max(-1, keepdims=True)], -1).astype(f)


def kernel(**inputs):
    import concourse.bacc as bacc
    from concourse.bass_utils import run_bass_kernel_spmd

    g = {k.replace("L0_", ""): np.asarray(v) for k, v in inputs.items()}
    feat = features()
    ft = np.zeros((NF, 2 * L), np.float32)
    ft[:, 0:2 * L - 1] = feat[np.abs(np.arange(2 * L - 1) - (L - 1))].T
    f0 = np.zeros((NF, 2), np.float32)
    f0[:, 1] = feat[0]

    def rows(w):
        a = np.zeros(w.shape[:-1] + (32,), w.dtype)
        for k in range(3):
            a[..., 8 * k:8 * k + 8] = w
        return a
    wq = rows(g["attn_b_Wq"].reshape(D, HB, DB)).reshape(D, 512)
    wk = rows(np.repeat(g["attn_b_Wk"][:, None, :], 4, 1)).reshape(D, 128)
    w_b = np.concatenate([wq, wk, g["attn_b_Wo"]], 1)
    bq = rows(g["attn_b_bq"].reshape(HB, DB)).reshape(4, 128)
    bk = rows(np.repeat(g["attn_b_bk"][None], 4, 0))
    bk[:, 24:26] = 1.0
    bias_b = np.concatenate([bq, bk.reshape(1, 128), np.zeros((1, 128), np.float32)], 0).T
    low = np.zeros((128, 2), np.float32)
    for q in range(4):
        low[32 * q + 8:32 * q + 16, 0] = -1.0
        low[32 * q + 16:32 * q + 24, 1] = -1.0
    wg, w1 = g["ffn_Wg"].T, g["ffn_W1"].transpose(2, 0, 1).reshape(D, E * 512)
    wg_last, w1_last = (np.concatenate([w[D - 1:D], np.zeros_like(w[0:1])], 0) for w in (wg, w1))
    arrays = {
        "q": g["attn_a_q"].reshape(B * L, D),
        "w_qs": g["attn_a_w_qs"], "w_ks": g["attn_a_w_ks"], "w_vs": g["attn_a_w_vs"],
        "w_rel": g["attn_a_w_rel_pos_k"], "w_out": g["attn_a_w_out"], "bo_a": g["attn_a_b_out"],
        "bias_a": np.concatenate([g["attn_a_rel_embed_bias"].reshape(H, DK), g["attn_a_rel_pos_bias"].reshape(H, DK)], 0).T,
        "feat": ft, "feat0": f0,
        "w_b": w_b, "wv_b": g["attn_b_Wv"], "bias_b": bias_b,
        "bvo_b": np.concatenate([g["attn_b_bv"], g["attn_b_bo"]]), "low": low,
        "wgt": np.concatenate([wg[0:D - 1], np.zeros_like(wg[0:1])], 0), "wgr": wg_last,
        "w1t": np.concatenate([w1[0:D - 1], g["ffn_b1"].reshape(1, -1)], 0), "w1r": w1_last, "wo_f": g["ffn_Wo"].T, "bo_f": g["ffn_bo"],
    }
    nc = bacc.Bacc("TRN2", target_bir_lowering=False, num_devices=1, dynamic_dma_scratch_size=1024)
    arrays = {k: np.ascontiguousarray(v) for k, v in arrays.items()}
    dram = {k: nc.dram_tensor(f"in_{k}", v.shape, mybir.dt.from_np(v.dtype), kind="ExternalInput").ap()
            for k, v in arrays.items()}
    dram["out"] = nc.dram_tensor("out_0", (B * L, D), F32, kind="ExternalOutput").ap()
    build(nc, dram)
    r = run_bass_kernel_spmd(nc, [{f"in_{k}": v for k, v in arrays.items()}], core_ids=[0])
    return np.asarray(r.results[0]["out_0"]).reshape(B, L, D)
```
